# Optimizing a Trainium2 kernel written in Bass

```python
import numpy as np
import jax
import jax.numpy as jnp

def _softmax(x, axis=-1):
    return jax.nn.softmax(x, axis=axis)

def _gelu(x):
    return jax.nn.gelu(x, approximate=True)

def _silu(x):
    return jax.nn.silu(x)

def _sigmoid(x):
    return jax.nn.sigmoid(x)

def _layernorm(x, axis=-1, eps=1e-05):
    m = jnp.mean(x, axis=axis, keepdims=True)
    v = jnp.var(x, axis=axis, keepdims=True)
    return (x - m) / jnp.sqrt(v + eps)

def _scatter_add(tgt, idx, src, axis=0):
    return tgt.at[idx].add(src)

def _segment_sum(src, seg, n):
    return jax.ops.segment_sum(src, seg, n)
kernel_name = 'mk_gnn_ffn_d1_gnn_r8_941657'

def setup_inputs(seed: int=0):
    np.random.seed(seed)
    _w = jnp.asarray

    def _rec_inputs():
        import jax
        import jax.numpy as jnp
        _gk = jax.random.key(seed)
        x = -8.776e-05 + 1 * jax.random.normal(jax.random.fold_in(_gk, 1), (6250, 256), jnp.float32)
        _s = jax.random.randint(jax.random.fold_in(_gk, 2), (100000,), 0, 6250, jnp.int32)
        _d = jax.random.randint(jax.random.fold_in(_gk, 3), (100000,), 0, 6250, jnp.int32)
        _loop = jnp.arange(6250, dtype=jnp.int32)
        src = jnp.concatenate([_s, _d, _loop])
        dst = jnp.concatenate([_d, _s, _loop])
        _o = jnp.argsort(dst, stable=True)
        src = src[_o]
        dst = dst[_o]
        edge_type_32 = jax.random.randint(jax.random.fold_in(_gk, 12), (206250,), 0, 32, jnp.int32)
        edge_weight1 = jax.random.uniform(jax.random.fold_in(_gk, 13), (206250, 1), jnp.float32, 0.0, 0.999998)
        return (x, src, dst, edge_type_32, edge_weight1)
    x, src, dst, edge_type_32, edge_weight1 = _rec_inputs()

    def _L0_gnn_setup():
        import jax, jax.numpy as jnp
        import numpy as np
        N_NODES = 2500
        N_EDGES = 40000
        IN_DIM = 256
        OUT_DIM = 256
        NUM_RELS = 32
        NUM_BASES = 8
        key = jax.random.key(seed)
        k1, k2, k3, k4, k5, k6, k7 = jax.random.split(key, 7)
        h = jax.random.normal(k1, (N_NODES, IN_DIM), dtype=jnp.float32)
        src = jax.random.randint(k2, (N_EDGES,), 0, N_NODES, dtype=jnp.int32)
        dst = jax.random.randint(k3, (N_EDGES,), 0, N_NODES, dtype=jnp.int32)
        rel_type = jax.random.randint(k4, (N_EDGES,), 0, NUM_RELS, dtype=jnp.int32)
        norm = jax.random.uniform(k5, (N_EDGES, 1), dtype=jnp.float32)
        scale_w = np.sqrt(2.0) * np.sqrt(6.0 / (IN_DIM + OUT_DIM))
        bases = jax.random.uniform(k6, (NUM_BASES, IN_DIM, OUT_DIM), dtype=jnp.float32, minval=-scale_w, maxval=scale_w)
        scale_c = np.sqrt(2.0) * np.sqrt(6.0 / (NUM_RELS + NUM_BASES))
        w_comp = jax.random.uniform(k7, (NUM_RELS, NUM_BASES), dtype=jnp.float32, minval=-scale_c, maxval=scale_c)
        return {'h': h, 'src': src, 'dst': dst, 'rel_type': rel_type, 'norm': norm, 'bases': bases, 'w_comp': w_comp}
    _L0_gnn_all = _L0_gnn_setup()
    _L0_gnn_in = {k: v for k, v in _L0_gnn_all.items() if k in ('bases', 'w_comp')}
    del _L0_gnn_all

    def _L0_ffn_setup():
        import jax, jax.numpy as jnp
        import numpy as np
        B, S, D, E, H, K = (4, 512, 256, 8, 512, 2)
        key = jax.random.key(seed)
        ks = jax.random.split(key, 6)
        x = jax.random.normal(ks[0], (B, S, D), jnp.float32)
        Wg = jax.random.normal(ks[1], (D, E), jnp.float32) * 0.02
        bg = jnp.zeros((E,), jnp.float32)
        W1 = jax.random.normal(ks[2], (E, D, H), jnp.float32) * 0.02
        b1 = jnp.zeros((E, H), jnp.float32)
        W2 = jax.random.normal(ks[3], (E, H, D), jnp.float32) * 0.02
        b2 = jnp.zeros((E, D), jnp.float32)
        return {'x': x, 'Wg': Wg, 'bg': bg, 'W1': W1, 'b1': b1, 'W2': W2, 'b2': b2}
    _L0_ffn_all = _L0_ffn_setup()
    _L0_ffn_in = {k: v for k, v in _L0_ffn_all.items() if k in ('Wg', 'bg', 'W1', 'b1', 'W2', 'b2')}
    del _L0_ffn_all
    return {'x': x, 'src': src, 'dst': dst, 'edge_type_32': edge_type_32, 'edge_weight1': edge_weight1, 'L0_gnn_bases': _L0_gnn_in['bases'], 'L0_gnn_w_comp': _L0_gnn_in['w_comp'], 'L0_ffn_Wg': _L0_ffn_in['Wg'], 'L0_ffn_bg': _L0_ffn_in['bg'], 'L0_ffn_W1': _L0_ffn_in['W1'], 'L0_ffn_b1': _L0_ffn_in['b1'], 'L0_ffn_W2': _L0_ffn_in['W2'], 'L0_ffn_b2': _L0_ffn_in['b2']}

def reference(x, src, dst, edge_type_32, edge_weight1, L0_gnn_bases, L0_gnn_w_comp, L0_ffn_Wg, L0_ffn_bg, L0_ffn_W1, L0_ffn_b1, L0_ffn_W2, L0_ffn_b2):
    import jax
    import jax.numpy as jnp

    def _L0_gnn_ref(h, src, dst, rel_type, norm, bases, w_comp):
        import jax, jax.numpy as jnp
        import numpy as np
        N_NODES = 2500
        N_EDGES = 40000
        IN_DIM = 256
        OUT_DIM = 256
        NUM_RELS = 32
        NUM_BASES = 8
        weight = jnp.einsum('rb,bio->rio', w_comp, bases)
        xw = jnp.einsum('ni,rio->nro', h, weight)
        msg = xw[src, rel_type] * norm
        out = jax.ops.segment_sum(msg, dst, num_segments=h.shape[0])
        return jax.nn.relu(out)

    def _L0_ffn_ref(x, Wg, bg, W1, b1, W2, b2):
        import jax, jax.numpy as jnp
        import numpy as np
        B, S, D, E, H, K = (4, 512, 256, 8, 512, 2)
        Bv, Sv, Dv = x.shape
        gate_scores = x @ Wg + bg
        _, idx = jax.lax.top_k(gate_scores, K)
        mask = jax.nn.one_hot(idx, E, dtype=x.dtype).sum(axis=-2)
        xf = x.reshape(-1, Dv)
        mf = mask.reshape(-1, E)
        h = jax.nn.gelu(jnp.einsum('td,edh->teh', xf, W1) + b1[None], approximate=False)
        y = jnp.einsum('teh,ehd->ted', h, W2) + b2[None]
        out = jnp.einsum('ted,te->td', y, mf)
        return out.reshape(Bv, Sv, Dv)
    x = x + _L0_gnn_ref(_layernorm(x, axis=-1), src, dst, edge_type_32, edge_weight1, L0_gnn_bases, L0_gnn_w_comp)
    x = x + _L0_ffn_ref(_layernorm(x, axis=-1)[None], L0_ffn_Wg, L0_ffn_bg, L0_ffn_W1, L0_ffn_b1, L0_ffn_W2, L0_ffn_b2)[0]
    return x

_drawn_inputs = setup_inputs


def setup_inputs(seed=0):
    import zlib

    import numpy as np

    out = dict(_drawn_inputs(seed))
    spreads = {'L0_ffn_bg': (0.0, 0.275), 'L0_ffn_b1': (0.0, 0.721), 'L0_ffn_b2': (0.0, 0.1)}
    factors = {}
    for name, (base, spread) in spreads.items():
        noise = np.random.default_rng([zlib.crc32(name.encode()), seed]).standard_normal(out[name].shape)
        drawn = base * np.exp(spread * noise) if base else spread * noise
        out[name] = jnp.asarray(drawn.astype(out[name].dtype))
    for name, factor in factors.items():
        out[name] = (out[name] * factor).astype(out[name].dtype)
    return out
```

```python
from contextlib import ExitStack

import concourse.bass as bass
from concourse import mybir

P = 128
ALU = mybir.AluOpType
ACT = mybir.ActivationFunctionType
F32 = mybir.dt.float32
I32 = mybir.dt.int32
U32 = mybir.dt.uint32
U16 = mybir.dt.uint16

EPS = 1e-5
WIN = 16
RING = 8
LAG = 4
SKIP = 1 << 24


def wait_apart(eng, sem, value, passed_by):
    value = value if isinstance(value, int) else eng.to_reg(value)
    eng.wait_ge(*passed_by)
    eng.wait_ge(sem, value)


class Tally:

    def __init__(self, eng, sem):
        self.eng, self.sem, self.base, self.n = eng, sem, 0, 0

    def mark(self, ins):
        ins.then_inc(self.sem, 1)
        self.n += 1

    def settle(self):
        self.eng.wait_ge(self.sem, self.base + self.n)

    def settle_apart(self, passed_by):
        wait_apart(self.eng, self.sem, self.base + self.n, passed_by)

    def enter(self, turn, per):
        self.start, self.per = self.base + self.n, per
        self.base, self.n = self.start + turn * per, 0

    def leave(self, turns):
        assert self.n == self.per, (self.n, self.per)
        self.base, self.n = self.start + turns * self.per, 0


def gnn_moe_layer(nc, x, src, dst, etype, eweight, bases, w_comp, Wg, bg, W1, b1, W2, b2, out):
    N, D = x.shape
    E = src.shape[0]
    B = bases.shape[0]
    R = w_comp.shape[0]
    NE, _, H = W1.shape
    NT = -(-N // P)
    LAST = N - (NT - 1) * P
    BPT = P // WIN
    NBLK = NT * BPT
    EPAIR = 2 * P
    NPAIR = -(-E // EPAIR)
    NTILE = 2 * NPAIR
    NCOL = -(-NTILE // P)
    DH = D // P
    HC = H // P
    GT = 64
    GM = GT // 4
    NGRP = -(-NTILE // GT)
    PER_E = -(-N // P)
    NSLOT = NE * PER_E
    NFFN = (2 * N + NE * (P - 1)) // P
    NFFN += NFFN % 2
    NSLOT_PAD = NSLOT + NFFN - (2 * N) // P + 1
    NSLOT_PAD += -NSLOT_PAD % 8
    assert D == 256 and B * WIN == P and R * 4 == P and NE == 8 and NSLOT_PAD <= 512 and E < 1 << 24

    h_dram = nc.dram_tensor("h_scratch", (N, D), F32, kind="Internal").ap()
    xn_dram = nc.dram_tensor("xn_scratch", (N, D), F32, kind="Internal").ap()

    with ExitStack() as ctx:
        def sb(name, shape, dt=F32):
            return ctx.enter_context(nc.sbuf_tensor(name, shape, dt))

        def sem(name):
            return ctx.enter_context(nc.semaphore(name))

        bank = [ctx.enter_context(nc.psum_tensor(f"bank{n}", [P, 512], F32)) for n in range(8)]
        acc, tr = bank[0:2], bank[2:4]
        ps_node, ps_small, ps_slot = bank[4], bank[5], bank[6]

        bases_sb = sb("bases_sb", [P, B, DH, D])
        ffn_w = sb("ffn_w", [P, NE * DH * H + NE * HC * D])
        w1_sb = ffn_w[:, 0:NE * DH * H]
        w2_sb = ffn_w[:, NE * DH * H:]
        xin = ffn_w[:, 0:NT * D].rearrange("p (t d) -> p t d", d=D)
        ONEHOT0 = NT * D
        onehot = ffn_w[:, ONEHOT0:ONEHOT0 + GM * P]
        WT0 = ONEHOT0 + GM * P
        wT = ffn_w[:, WT0:WT0 + NCOL * P]
        assert WT0 + NCOL * P <= NE * DH * H + NE * HC * D

        coef = sb("coef", [P, NTILE * B])
        RAW = NCOL * P
        raw_i = [coef[:, k * RAW:(k + 1) * RAW].bitcast(I32) for k in range(2)]
        raw_f = [coef[:, k * RAW:(k + 1) * RAW] for k in range(2, 5)]
        passed = coef[:, 5 * RAW:5 * RAW + 7 * NBLK].rearrange("p (c j) -> p c j", j=NBLK)
        ROW0 = 5 * RAW + 7 * NBLK
        row_i, row_f = coef[0:1, ROW0:ROW0 + NPAIR].bitcast(I32), coef[0:1, ROW0 + NPAIR:ROW0 + 2 * NPAIR]
        assert ROW0 + 2 * NPAIR <= NTILE * B
        used = [0]

        def late(n):
            used[0] += n
            assert used[0] <= NTILE * B
            return coef[:, used[0] - n:used[0]]

        b1_bc, b2_bc = late(NE * H), late(NE * D)
        hid, act, actT, xbT = late(H), late(H), late(H), late(D)
        slot_f = late(2 * NSLOT_PAD).rearrange("p (o c) -> p o c", o=2)
        slot_i = late(2 * NSLOT_PAD).bitcast(I32).rearrange("p (c o) -> p c o", o=2)
        y_sb, xb = [late(D), late(D)], [late(D), late(D)]

        dstT = sb("dstT", [P, NCOL * P])
        srcT = sb("srcT", [P, NCOL * P], I32)
        nodes = sb("nodes", [P, NBLK * WIN], U16)
        ring = sb("ring", [P, RING * 2 * D])
        S = sb("S", [P, 2, P])
        blk = sb("blk", [P, 2, D])
        aggT = sb("aggT", [P, DH * B * P])
        bases_flat = bases_sb[:, :, :, :].rearrange("p b h o -> p (b h o)")
        types = [bases_flat[:, n * GM * P:(n + 1) * GM * P].bitcast(I32) for n in range(2)]
        idx = sb("idx", [P, 2, 2 * RING], I32)
        ident = sb("ident", [P, P])
        lower = sb("lower", [P, P])
        ones = sb("ones", [P, P])
        zeros = sb("zeros", [P, D])
        comp4 = sb("comp4", [P, 4 * B])
        part = sb("part", [P, 2], I32)
        partf = sb("partf", [P, 1])
        pair_end = sb("pair_end", [P, 7], I32)
        pair_endf = sb("pair_endf", [P, 7])
        Mt = sb("Mt", [1, NBLK + 8], I32)
        free_at = sb("free_at", [1, NPAIR + LAG + 4], I32)
        stats = sb("stats", [P, 8, 6])
        mv = sb("mv", [P, NT, 2])
        mv7 = sb("mv7", [P, 7, 2])
        rs = sb("rs", [P, NT])
        xt = sb("xt", [P, D])
        x1 = sb("x1", [P, D])
        xn = sb("xn", [P, D])
        xnT = sb("xnT", [P, D])
        bst = sb("bst", [P, 6])
        bmv = sb("bmv", [P, 2])
        brs = sb("brs", [P, 2])
        Wg_sb = sb("Wg_sb", [P, DH, NE])
        bg_sb = sb("bg_sb", [P, NE])
        gate = sb("gate", [P, 2, NE])
        top = sb("top", [P, NE], U32)
        topf = sb("topf", [P, 2])
        pick = sb("pick", [P, 3, NE])
        count = sb("count", [P, NE])
        place = sb("place", [P, NE])
        scr = sb("scr", [P, NE])
        rank = sb("rank", [P, 2])
        rank_i = sb("rank_i", [P, 3, 2], I32)
        rank_f = sb("rank_f", [P, 2, 2])
        slot_oh = sb("slot_oh", [P, 2, P])
        col_id = sb("col_id", [P, 2, NSLOT])
        token = sb("token", [P, 1])
        nb = sb("nb", [P, 3, NE])
        nb_i = sb("nb_i", [P, NE], I32)
        blkrow = sb("blkrow", [P, 3, NFFN])
        blk_e = sb("blk_e", [1, NFFN], I32)
        blk_c = sb("blk_c", [1, NFFN], I32)
        gidx = sb("gidx", [P, 2, 2], I32)
        sidx = sb("sidx", [P, 2, 2], I32)

        pads = sem("pads")
        raw_in = [sem(f"raw_in{k}") for k in range(3)]
        ends_in = sem("ends_in")
        x_in = sem("x_in")
        consts = sem("consts")
        small_in = sem("small_in")
        bases_in = sem("bases_in")
        conv = sem("conv")
        batch = sem("batch")
        batch_out = sem("batch_out")
        var_ok, std_ok, rs_ok = sem("var_ok"), sem("std_ok"), sem("rs_ok")
        norm_d, norm_p = sem("norm_d"), sem("norm_p")
        h_out = sem("h_out")
        passed_ok, M_ok = sem("passed_ok"), sem("M_ok")
        tables = sem("tables")
        type_in = [sem("type_in0"), sem("type_in1")]
        oh_ok, oh_used, coef_ps, coef_ok = sem("oh_ok"), sem("oh_used"), sem("coef_ps"), sem("coef_ok")
        w_in, b_in = sem("w_in"), sem("b_in")
        idx_ok = sem("idx_ok")
        ring_in = [sem(f"ring_in{k}") for k in range(RING)]
        gathered = sem("gathered")
        released = sem("released")
        S_ok = [sem("S_ok0"), sem("S_ok1")]
        S_used = [sem("S_used0"), sem("S_used1")]
        blk_ok = sem("blk_ok")
        acc_zero = sem("acc_zero")
        tr_ok, aggT_ok = sem("tr_ok"), sem("aggT_ok")
        xf_ok = sem("xf_ok")
        xt_in, x1_ok, x1_out = sem("xt_in"), sem("x1_ok"), sem("x1_out")
        sd_ok, xn_ok, xn_out = sem("sd_ok"), sem("xn_ok"), sem("xn_out")
        xnT_ps, xnT_ok, gate_ps = sem("xnT_ps"), sem("xnT_ok"), sem("gate_ps")
        pick_ok, rank_ps, oh2_ok, map_ok = sem("pick_ok"), sem("rank_ps"), sem("oh2_ok"), sem("map_ok")
        dve_own, act_own, pool_own = sem("dve_own"), sem("act_own"), sem("pool_own")
        slots_ok = sem("slots_ok")
        g_idx_ok, s_idx_ok = sem("g_idx_ok"), sem("s_idx_ok")
        xb_in = [sem("xb_in0"), sem("xb_in1")]
        xbT_ps, xbT_ok, hid_ps, hid_ok = sem("xbT_ps"), sem("xbT_ok"), sem("hid_ps"), sem("hid_ok")
        act_ok, actT_ps, actT_ok, y_ps, y_ok = (sem("act_ok"), sem("actT_ps"), sem("actT_ok"),
                                                sem("y_ps"), sem("y_ok"))
        y_out = sem("y_out")

        block = ctx.enter_context(nc.Block())

        e_full = (E // (P * P)) * P * P
        e_rows = (E - e_full) // P
        e_rest = E - e_full - e_rows * P
        lists = [src, dst, eweight.rearrange("e o -> (e o)")]
        raw_to = [raw_i[0], raw_i[1], raw_f[2]]
        raw_fl = [raw_f[0], raw_f[1], raw_f[2]]
        batches = [(k, c, min(4, NCOL - c)) for k in range(3) for c in range(0, NCOL, 4)]
        full_pairs = E // EPAIR
        pc, pr = full_pairs // P, full_pairs % P

        def steps_of_tile(r):
            return LAST if isinstance(r, int) and r == NT - 1 else P

        @block.sync
        def _(sp):
            sp.wait_ge(pads, 6)
            for k in range(3):
                to = raw_to[k].rearrange("p (c e) -> p c e", e=P)
                c = e_full // (P * P)
                sp.dma_start(to[:, 0:c, :], lists[k][0:e_full].rearrange("(c p e) -> p c e", p=P, e=P)
                             ).then_inc(raw_in[k], 16)
                sp.dma_start(to[0:e_rows, c, :], lists[k][e_full:E - e_rest].rearrange("(p e) -> p e", e=P)
                             ).then_inc(raw_in[k], 16)
                sp.dma_start(to[e_rows:e_rows + 1, c, 0:e_rest],
                             lists[k][E - e_rest:E].rearrange("(o e) -> o e", o=1)).then_inc(raw_in[k], 16)
            full = (NT - 1) // 7 * 7
            for c in range(0, full, 7):
                sp.dma_start(xin[:, c:c + 7, :], x[c * P:(c + 7) * P, :].rearrange("(t p) d -> p t d", p=P)
                             ).then_inc(x_in, 16)
            sp.dma_start(xin[:, full:NT - 1, :],
                         x[full * P:(NT - 1) * P, :].rearrange("(t p) d -> p t d", p=P)).then_inc(x_in, 16)
            sp.dma_start(xin[0:LAST, NT - 1, :], x[(NT - 1) * P:N, :]).then_inc(x_in, 16)
            ends = dst[0:full_pairs * EPAIR].rearrange("(m e) -> m e", e=EPAIR)[:, EPAIR - 1:EPAIR]
            with nc.allow_non_contiguous_dma(reason="one destination of each pair"):
                sp.dma_start(pair_end[:, 0:pc], ends[0:pc * P, :].rearrange("(c p) o -> p (c o)", p=P)
                             ).then_inc(ends_in, 16)
                sp.dma_start(pair_end[0:pr, pc:pc + 1], ends[pc * P:, :]).then_inc(ends_in, 16)
                sp.dma_start(row_i[0:1, 0:full_pairs], ends.rearrange("m o -> o m")).then_inc(ends_in, 16)
            sp.wait_ge(consts, 6)
            for q in range(4):
                sp.dma_start(comp4[R * q:R * q + R, B * q:B * q + B], w_comp).then_inc(small_in, 16)
            sp.dma_start(Wg_sb[:, :, :], Wg.rearrange("(h p) e -> p h e", p=P)).then_inc(small_in, 16)
            sp.dma_start(bg_sb[:, :], bg.rearrange("(o e) -> o e", o=1).to_broadcast([P, NE])
                         ).then_inc(small_in, 16)
            sp.wait_ge(norm_p, NT - NT // 2)
            sp.wait_ge(norm_d, NT // 2)
            sp.dma_start(h_dram[0:(NT - 1) * P, :].rearrange("(t p) d -> p t d", p=P), xin[:, 0:NT - 1, :]
                         ).then_inc(h_out, 16)
            sp.dma_start(h_dram[(NT - 1) * P:N, :], xin[0:LAST, NT - 1, :]).then_inc(h_out, 16)

            def load_types(g, par, quarters, first):
                if not first:
                    sp.wait_ge(oh_ok, g - 1)
                for q in range(quarters):
                    n = min(GM * P, E - g * (GT * P) - q * GM * P) if isinstance(g, int) else GM * P
                    sp.dma_start(types[par][R * q:R * q + R, 0:n],
                                 etype[bass.ds(g * (GT * P) + q * GM * P, n)].rearrange("(o n) -> o n", o=1)
                                 .to_broadcast([R, n])).then_inc(type_in[par], 16)

            load_types(0, 0, 4, True)
            load_types(1, 1, 4, True)
            with sp.Fori(1, NGRP // 2 - 1) as i:
                for par in range(2):
                    load_types(i * 2 + par, par, 4, False)
            load_types(NGRP - 2, 0, 4, False)
            load_types(NGRP - 1, 1, 1, False)
            sp.wait_ge(oh_ok, NGRP)
            for b in range(B):
                sp.dma_start(bases_sb[:, b, :, :], bases[b].rearrange("(h p) o -> p h o", p=P)
                             ).then_inc(bases_in, 16)

            def relay(slot, turn, m, lagged):
                sp.wait_ge(ring_in[slot], turn * 32 + 32)
                sp.sem_inc(gathered, 1)
                if lagged:
                    at = sp.value_load(free_at[0:1, bass.ds(m, 1)], min_val=1, max_val=NPAIR + NBLK + 2)
                    sp.wait_ge(S_used[1], at)
                    sp.sem_inc(released, 1)

            sp.wait_ge(tables, 2)
            for m in range(RING):
                relay(m, 0, m, m >= LAG)
            with sp.Fori(1, NPAIR // RING) as turn:
                for k in range(RING):
                    relay(k, turn, turn * RING + k, True)
            for k in range(NPAIR % RING):
                relay(k, NPAIR // RING, NPAIR // RING * RING + k, True)

        @block.gpsimd
        def _(pool):
            g = nc.gpsimd
            for k, v in ((0, 0), (1, NBLK * WIN - 1)):
                g.memset(raw_i[k][:, (NCOL - 1) * P:], v).then_inc(pads, 1)
            g.memset(raw_f[2][:, (NCOL - 1) * P:], 0.0).then_inc(pads, 1)
            g.memset(pair_end[:, :], NBLK * WIN - 1).then_inc(pads, 1)
            g.memset(row_i, NBLK * WIN - 1).then_inc(pads, 1)
            g.memset(xin[:, NT - 1, :], 0.0).then_inc(pads, 1)
            g.memset(ones[:, :], 1.0).then_inc(pool_own, 1)
            g.memset(zeros[:, :], 0.0).then_inc(consts, 1)
            g.memset(comp4[:, :], 0.0).then_inc(consts, 1)
            g.iota(nodes[:, :], [[1, NBLK * WIN]], base=0, channel_multiplier=0).then_inc(consts, 1)
            g.iota(part[:, 0:1], [[0, 1]], base=0, channel_multiplier=1).then_inc(consts, 1)
            pool.wait_ge(pool_own, 1)
            g.affine_select(out=ident[:, :], in_=ones[:, :], compare_op=ALU.is_equal, fill=0.0, base=0,
                            pattern=[[-1, P]], channel_multiplier=1).then_inc(consts, 1)
            g.affine_select(out=lower[:, :], in_=ones[:, :], compare_op=ALU.is_gt, fill=0.0, base=0,
                            pattern=[[1, P]], channel_multiplier=-1).then_inc(consts, 1)
            pool.wait_ge(rs_ok, 1)
            for t in range(NT // 2, NT):
                g.tensor_scalar(xin[:, t, :], xin[:, t, :], mv[:, t, 0:1], rs[:, t:t + 1],
                                ALU.subtract, ALU.mult).then_inc(norm_p, 1)

            pool.wait_ge(batch_out, len([0 for k, _, _ in batches if k == 0]))
            pool.wait_ge(h_out, 32)
            turns = NPAIR // (2 * RING)

            def gathers(half, m0, n, copies, first):
                if not first:
                    pool.wait_ge(released, m0 - RING + 1)
                g.tensor_copy(idx[:, half, 0:2 * n], srcT[:, bass.ds(m0 * 2, 2 * n)]).then_inc(idx_ok, 1)
                wait_apart(pool, idx_ok, copies + 1, (h_out, 32))
                for k in range(n):
                    if not first:
                        wait_apart(pool, released, m0 + k - RING + 1, (h_out, 32))
                    for t in range(2):
                        at = (k * 2 + t) * D
                        g.indirect_dma_start(
                            out=ring[:, at:at + D], out_offset=None, in_=h_dram,
                            in_offset=bass.IndirectOffsetOnAxis(ap=idx[:, half, 2 * k + t:2 * k + t + 1], axis=0)
                        ).then_inc(ring_in[k], 16)

            gathers(0, 0, RING, 0, True)
            gathers(1, RING, RING, 1, False)
            with pool.Fori(1, turns) as turn:
                gathers(0, turn * 2 * RING, RING, turn * 2, False)
                gathers(1, turn * 2 * RING + RING, RING, turn * 2 + 1, False)
            rest = NPAIR - turns * 2 * RING
            assert 0 < rest <= RING
            gathers(0, turns * 2 * RING, rest, turns * 2, False)

            pool.wait_ge(slots_ok, 1)
            pool.wait_ge(xn_out, 16 * NT + 16)
            pool.wait_ge(x1_out, 16 * NT + 16)
            pool.wait_ge(w_in, 16 * 2 * NE)

            def fetch(k, par):
                c = pool.value_load(blk_c[0:1, bass.ds(k, 1)], min_val=0, max_val=NSLOT_PAD - 1)
                g.tensor_copy(gidx[:, par, :], slot_i[:, bass.ds(c, 1), :].rearrange("p a b -> p (a b)")
                              ).then_inc(g_idx_ok, 1)
                wait_apart(pool, g_idx_ok, k + 1, (slots_ok, 1))
                g.indirect_dma_start(
                    out=xb[par], out_offset=None, in_=xn_dram,
                    in_offset=bass.IndirectOffsetOnAxis(ap=gidx[:, par, 0:1], axis=0)).then_inc(xb_in[par], 16)

            def add_rows(k, par):
                c = pool.value_load(blk_c[0:1, bass.ds(k, 1)], min_val=0, max_val=NSLOT_PAD - 1)
                g.tensor_copy(sidx[:, par, :], slot_i[:, bass.ds(c, 1), :].rearrange("p a b -> p (a b)")
                              ).then_inc(s_idx_ok, 1)
                pool.wait_ge(s_idx_ok, k + 1)
                pool.wait_ge(y_ok, k + 1)
                if not (isinstance(k, int) and k == 0):
                    wait_apart(pool, y_out, k * 16, (slots_ok, 1))
                g.indirect_dma_start(
                    out=out, out_offset=bass.IndirectOffsetOnAxis(ap=sidx[:, par, 1:2], axis=0),
                    in_=y_sb[par], in_offset=None, bounds_check=N - 1, oob_is_err=False,
                    compute_op=ALU.add).then_inc(y_out, 16)

            fetch(0, 0)
            fetch(1, 1)

            def turn_of(k, par, first, last):
                if not last:
                    pool.wait_ge(xbT_ps, k + 1)
                    fetch(k + 2, par)
                add_rows(k, par)

            turn_of(0, 0, True, False)
            turn_of(1, 1, True, False)
            with pool.Fori(1, NFFN // 2 - 1) as t:
                for par in range(2):
                    turn_of(t * 2 + par, par, False, False)
            for par in range(2):
                turn_of(NFFN - 2 + par, par, False, True)
            pool.wait_ge(y_out, NFFN * 16)

        @block.tensor
        def _(pe):
            t = nc.tensor
            pe.wait_ge(consts, 6)
            for n, (k, c, w) in enumerate(batches):
                if c == 0:
                    if k < 2:
                        pe.wait_ge(conv, k + 1)
                    else:
                        pe.wait_ge(raw_in[2], 48)
                if n >= 8:
                    pe.wait_ge(batch_out, n - 7)
                for u in range(w):
                    mm = t.transpose(bank[n % 8][:, u * P:(u + 1) * P],
                                     raw_fl[k][:, (c + u) * P:(c + u + 1) * P], ident[:, :])
                mm.then_inc(batch, 1)
            pe.wait_ge(passed_ok, 7)
            pe.wait_ge(batch_out, len(batches))
            for c in range(7):
                mm = t.matmul(bank[4][:, 0:NBLK], ones[:, :], passed[:, c, :], start=(c == 0), stop=(c == 6))
            mm.then_inc(M_ok, 1)
            pe.wait_ge(small_in, 96)

            def comps(g, par, first):
                pe.wait_ge(oh_ok, g + 1)
                if not first:
                    pe.wait_ge(coef_ok, g - 1)
                for m in range(GM):
                    mm = t.matmul(bank[par][:, m * 4 * B:(m + 1) * 4 * B], onehot[:, m * P:(m + 1) * P],
                                  comp4[:, :], start=True, stop=True)
                mm.then_inc(coef_ps, 1)

            comps(0, 0, True)
            comps(1, 1, True)
            with pe.Fori(1, NGRP // 2) as i:
                for par in range(2):
                    comps(i * 2 + par, par, False)
            assert NGRP % 2 == 0

            pe.wait_ge(bases_in, 16 * B)
            pe.wait_ge(coef_ok, NGRP)
            t.matmul(ps_small[:, 0:NE], ones[:, :], ones[:, 0:NE], start=True, stop=True).then_inc(S_used[0], 1)
            t.matmul(ps_small[:, 0:NE], ones[:, :], ones[:, 0:NE], start=True, stop=True).then_inc(S_used[1], 1)
            pe.wait_ge(tables, 2)

            def steps(j, jj, lo, hi):
                wait_apart(pe, acc_zero, j + 1, (tables, 2))
                with pe.Fori(lo, hi + 1) as m:
                    pe.wait_ge(gathered, m + 1)
                    for u in range(2):
                        pe.wait_ge(S_ok[u], m + j + 1)
                        t.matmul(acc[jj % 2][:, 0:D], S[:, u, :],
                                 ring[:, bass.ds((m % RING) * (2 * D) + u * D, D)],
                                 start=False, stop=False, skip_group_check=True).then_inc(S_used[u], 1)

            def turn_block(j, par):
                pe.wait_ge(blk_ok, j + 1)
                pe.wait_ge(aggT_ok, j + 1)
                for h in range(DH):
                    mm = t.transpose(tr[par][:, h * P:(h + 1) * P], blk[:, par, h * P:(h + 1) * P], ident[:, :])
                mm.then_inc(tr_ok, 1)

            def transform(r):
                pe.wait_ge(aggT_ok, r * BPT + BPT + 2)
                pe.wait_ge(x1_ok, r + 1)
                for n in range(B * DH):
                    b, h = n // DH, n % DH
                    mm = t.matmul(ps_node[:, 0:D], aggT[:, (h * B + b) * P:(h * B + b + 1) * P],
                                  bases_sb[:, b, h, :], start=(n == 0), stop=(n == B * DH - 1))
                mm.then_inc(xf_ok, 1)

            def node_work(jj, r):
                if jj == 4:
                    pe.wait_ge(xn_ok, r + 1)
                    for h in range(DH):
                        mm = t.transpose(ps_small[:, h * P:(h + 1) * P], xn[:, h * P:(h + 1) * P], ident[:, :])
                    mm.then_inc(xnT_ps, 1)
                if jj == 5:
                    pe.wait_ge(xnT_ok, r + 1)
                    for h in range(DH):
                        mm = t.matmul(ps_small[:, D:D + NE], xnT[:, h * P:(h + 1) * P], Wg_sb[:, h, :],
                                      start=(h == 0), stop=(h == DH - 1))
                    mm.then_inc(gate_ps, 1)
                if jj == 6:
                    k = steps_of_tile(r)
                    pe.wait_ge(pick_ok, r + 1)
                    t.matmul(ps_small[:, 272:272 + NE], lower[0:k, :], pick[0:k, 2, :], start=True, stop=True)
                    t.matmul(ps_small[:, 288:288 + NE], ones[0:k, :], pick[0:k, 2, :], start=True, stop=True
                             ).then_inc(rank_ps, 1)
                if jj == 7:
                    k = steps_of_tile(r)
                    pe.wait_ge(oh2_ok, r + 1)
                    for c in range(2):
                        mm = t.matmul(ps_slot[:, 0:NSLOT], slot_oh[0:k, c, :], col_id[0:k, c, :],
                                      start=False, stop=False, skip_group_check=True)
                    mm.then_inc(map_ok, 1)

            def tile(i, first):
                lo = pe.value_load(Mt[0:1, bass.ds(i * BPT, 1)], min_val=0, max_val=NPAIR - 1)
                for jj in range(BPT):
                    j = i * BPT + jj
                    hi = pe.value_load(Mt[0:1, bass.ds(j + 1, 1)], min_val=0, max_val=NPAIR - 1)
                    steps(j, jj, lo, hi)
                    lo = hi
                    if jj == 1 and not first:
                        transform(i - 1)
                    if not (first and jj == 0):
                        turn_block(j - 1, (jj - 1) % 2)
                    if not first:
                        node_work(jj, i - 1)

            pe.sem_inc(map_ok, 1)
            tile(0, True)
            with pe.Fori(1, NT) as i:
                tile(i, False)
            turn_block(NBLK - 1, 1)
            transform(NT - 1)
            for jj in range(BPT):
                node_work(jj, NT - 1)

            pe.wait_ge(slots_ok, 1)
            pe.wait_ge(w_in, 16 * 2 * NE)
            pe.wait_ge(acc_zero, NBLK + 2)
            ps_h, ps_y, ps_xT, ps_aT = bank[0], bank[1], bank[2], bank[3]

            def rows_T(k, par, turn):
                pe.wait_ge(xb_in[par], turn * 16 + 16)
                if not (isinstance(k, int) and k == 0):
                    pe.wait_ge(xbT_ok, k)
                for h in range(DH):
                    mm = t.transpose(ps_xT[:, h * P:(h + 1) * P], xb[par][:, h * P:(h + 1) * P], ident[:, :])
                mm.then_inc(xbT_ps, 1)

            def expert(k):
                return pe.value_load(blk_e[0:1, bass.ds(k, 1)], min_val=0, max_val=NE - 1)

            def up(k, e):
                pe.wait_ge(xbT_ok, k + 1)
                if not (isinstance(k, int) and k == 0):
                    pe.wait_ge(hid_ok, k)
                for h in range(DH):
                    mm = t.matmul(ps_h[:, 0:H], xbT[:, h * P:(h + 1) * P],
                                  w1_sb[:, bass.ds(e * (DH * H) + h * H, H)], start=(h == 0), stop=(h == DH - 1))
                mm.then_inc(hid_ps, 1)

            def hidden_T(k):
                pe.wait_ge(act_ok, k + 1)
                if not (isinstance(k, int) and k == 0):
                    pe.wait_ge(actT_ok, k)
                for c in range(HC):
                    mm = t.transpose(ps_aT[:, c * P:(c + 1) * P], act[:, c * P:(c + 1) * P], ident[:, :])
                mm.then_inc(actT_ps, 1)

            def down(k, e):
                pe.wait_ge(actT_ok, k + 1)
                if not (isinstance(k, int) and k == 0):
                    pe.wait_ge(y_ok, k)
                for c in range(HC):
                    mm = t.matmul(ps_y[:, 0:D], actT[:, c * P:(c + 1) * P],
                                  w2_sb[:, bass.ds(e * (HC * D) + c * D, D)], start=(c == 0), stop=(c == HC - 1))
                mm.then_inc(y_ps, 1)

            def turn_of(k, par, turn, ahead):
                e = expert(k)
                hidden_T(k)
                if ahead >= 1:
                    up(k + 1, expert(k + 1))
                if ahead >= 2:
                    rows_T(k + 2, par, turn + 1)
                down(k, e)

            rows_T(0, 0, 0)
            up(0, expert(0))
            rows_T(1, 1, 0)
            turn_of(0, 0, 0, 2)
            turn_of(1, 1, 0, 2)
            with pe.Fori(1, NFFN // 2 - 1) as i:
                for par in range(2):
                    turn_of(i * 2 + par, par, i, 2)
            turn_of(NFFN - 2, 0, NFFN // 2 - 1, 1)
            turn_of(NFFN - 1, 1, NFFN // 2 - 1, 0)

        @block.scalar
        def _(act_):
            a = nc.scalar
            for n, (k, c, w) in enumerate(batches):
                act_.wait_ge(batch, n + 1)
                to = (srcT, dstT, wT)[k][:, c * P:(c + w) * P]
                a.activation(to, bank[n % 8][:, 0:w * P], ACT.Copy).then_inc(batch_out, 1)
            act_.wait_ge(var_ok, 1)
            a.activation(rs[:, :], mv[:, :, 1], ACT.Sqrt).then_inc(std_ok, 1)
            act_.wait_ge(h_out, 32)
            act_.wait_ge(coef_ok, NGRP)
            for e in range(NE):
                act_.dma_start(w1_sb[:, e * DH * H:(e + 1) * DH * H].rearrange("p (h n) -> p h n", n=H),
                               W1[e].rearrange("(h p) n -> p h n", p=P)).then_inc(w_in, 16)
                act_.dma_start(w2_sb[:, e * HC * D:(e + 1) * HC * D].rearrange("p (c n) -> p c n", n=D),
                               W2[e].rearrange("(c p) n -> p c n", p=P)).then_inc(w_in, 16)
            act_.wait_ge(consts, 6)
            for n in range(2):
                a.activation(acc[n][:, 0:D], zeros[:, :], ACT.Copy).then_inc(acc_zero, 1)
            act_.wait_ge(tables, 2)

            def block_out(j, jj, hi):
                act_.wait_ge(S_used[1], hi + (j + 2))
                if not (isinstance(j, int) and j < 2):
                    act_.wait_ge(tr_ok, j - 1)
                a.activation(blk[:, jj % 2, :], acc[jj % 2][:, 0:D], ACT.Copy).then_inc(blk_ok, 1)
                act_.wait_ge(blk_ok, j + 1)
                a.activation(acc[jj % 2][:, 0:D], zeros[:, :], ACT.Copy).then_inc(acc_zero, 1)

            def block_T(j, jj, prev):
                act_.wait_ge(tr_ok, j + 1)
                if jj == 0 and prev is not None:
                    act_.wait_ge(xf_ok, prev + 1)
                to = aggT[:, :].rearrange("p (g n) -> p g n", n=P)[:, :, jj * WIN:(jj + 1) * WIN]
                a.activation(to, tr[jj % 2][:, 0:D].rearrange("p (g n) -> p g n", n=WIN), ACT.Copy
                             ).then_inc(aggT_ok, 1)

            def node_work(jj, r):
                k = steps_of_tile(r)
                rows = bass.ds(r * P, k)
                if jj == 0:
                    act_.wait_ge(x1_ok, r + 1)
                    act_.dma_start(xt[0:k, :], x[rows, :]).then_inc(xt_in, 16)
                if jj == 2:
                    act_.wait_ge(x1_ok, r + 2)
                    act_.dma_start(out[rows, :], x1[0:k, :]).then_inc(x1_out, 16)
                    act_.wait_ge(sd_ok, r * 2 + 1)
                    a.activation(brs[:, 1:2], brs[:, 0:1], ACT.Sqrt).then_inc(sd_ok, 1)
                if jj == 4:
                    act_.wait_ge(xn_ok, r + 1)
                    act_.dma_start(xn_dram[rows, :], xn[0:k, :]).then_inc(xn_out, 16)
                    act_.wait_ge(xnT_ps, r + 1)
                    a.activation(xnT[:, :], ps_small[:, 0:D], ACT.Copy).then_inc(xnT_ok, 1)

            def tile(i, first):
                for jj in range(BPT):
                    j = i * BPT + jj
                    hi = act_.value_load(Mt[0:1, bass.ds(j + 1, 1)], min_val=0, max_val=NPAIR - 1)
                    block_out(j, jj, hi)
                    if jj > 0:
                        block_T(j - 1, jj - 1, None if first else i - 1)
                    elif not first:
                        block_T(j - 1, BPT - 1, None)
                    if not first:
                        node_work(jj, i - 1)

            act_.sem_inc(aggT_ok, 2)
            act_.sem_inc(x1_out, 16)
            act_.sem_inc(xn_out, 16)
            tile(0, True)
            with act_.Fori(1, NT) as i:
                tile(i, False)
            block_T(NBLK - 1, BPT - 1, None)
            for jj in range(BPT):
                node_work(jj, NT - 1)

            act_.wait_ge(S_used[1], NPAIR + NBLK)
            act_.dma_start(b1_bc, b1.rearrange("(o e) n -> o (e n)", o=1).to_broadcast([P, NE * H])
                           ).then_inc(b_in, 16)
            act_.dma_start(b2_bc, b2.rearrange("(o e) n -> o (e n)", o=1).to_broadcast([P, NE * D])
                           ).then_inc(b_in, 16)
            act_.wait_ge(slots_ok, 1)

            def turn_T(k):
                act_.wait_ge(xbT_ps, k + 1)
                if not (isinstance(k, int) and k == 0):
                    act_.wait_ge(hid_ps, k)
                a.activation(xbT, bank[2][:, 0:D], ACT.Copy).then_inc(xbT_ok, 1)

            def turn_of(k, last):
                act_.wait_ge(hid_ok, k + 1)
                if not (isinstance(k, int) and k == 0):
                    act_.wait_ge(actT_ps, k)
                a.activation(act, hid, ACT.Gelu).then_inc(act_ok, 1)
                act_.wait_ge(actT_ps, k + 1)
                if not (isinstance(k, int) and k == 0):
                    act_.wait_ge(y_ps, k)
                a.activation(actT, bank[3][:, 0:H], ACT.Copy).then_inc(actT_ok, 1)
                if last < 2:
                    turn_T(k + 2) if last == 0 else None

            turn_T(0)
            turn_T(1)
            turn_of(0, 0)
            with act_.Fori(1, NFFN - 2) as k:
                turn_of(k, 0)
            turn_of(NFFN - 2, 1)
            turn_of(NFFN - 1, 1)

        @block.vector
        def _(dve):
            v = nc.vector
            own = Tally(dve, dve_own)
            dve.wait_ge(raw_in[0], 48)
            v.tensor_copy(raw_fl[0], raw_i[0]).then_inc(conv, 1)
            dve.wait_ge(raw_in[1], 48)
            v.tensor_copy(raw_fl[1], raw_i[1]).then_inc(conv, 1)

            dve.wait_ge(x_in, 16 * 8)
            dve.wait_ge(pads, 6)

            def statistics(t0):
                for u in range(7):
                    own.mark(v.bn_stats(stats[:, u, :], xin[:, bass.ds(t0 + u, 1), :].rearrange("p a d -> p (a d)")))
                own.settle_apart((pads, 6))
                for u in range(7):
                    own.mark(v.bn_aggr(mv7[:, u, :], stats[:, u, :]))
                own.settle()
                own.mark(v.tensor_copy(mv[:, bass.ds(t0, 7), :], mv7[:, :, :]))
                own.settle()

            assert NT % 7 == 0
            with dve.Fori(0, NT // 7) as i:
                own.enter(i, 15)
                statistics(i * 7)
                own.leave(NT // 7)
            v.tensor_scalar(mv[:, :, 1], mv[:, :, 1], EPS, None, ALU.add).then_inc(var_ok, 1)
            dve.wait_ge(std_ok, 1)
            v.reciprocal(rs[:, :], rs[:, :]).then_inc(rs_ok, 1)
            dve.wait_ge(rs_ok, 1)
            for n in range(NT // 2):
                v.tensor_scalar(xin[:, n, :], xin[:, n, :], mv[:, n, 0:1], rs[:, n:n + 1],
                                ALU.subtract, ALU.mult).then_inc(norm_d, 1)

            dve.wait_ge(ends_in, 48)
            own.mark(v.tensor_scalar(pair_end[:, :], pair_end[:, :], 4, None, ALU.arith_shift_right))
            own.mark(v.tensor_scalar(row_i, row_i, 4, None, ALU.arith_shift_right))
            own.settle()
            own.mark(v.tensor_copy(pair_endf[:, :], pair_end[:, :]))
            own.mark(v.tensor_copy(row_f, row_i))
            own.mark(v.memset(Mt[:, :], 0))
            own.mark(v.memset(free_at[:, :], 1))
            own.settle()
            dve.wait_ge(consts, 6)
            for c in range(7):
                v.tensor_scalar(passed[:, c, :], nodes[:, 0:NBLK], pair_endf[:, c:c + 1], None, ALU.is_ge
                                ).then_inc(passed_ok, 1)
            v.scalar_tensor_tensor(free_at[0:1, LAG:LAG + NPAIR], row_f[0:1, :], 2.0, nodes[0:1, 0:NPAIR],
                                   ALU.add, ALU.add).then_inc(tables, 1)
            dve.wait_ge(M_ok, 1)
            v.tensor_scalar(Mt[0:1, 1:NBLK + 1], bank[4][0:1, 0:NBLK], float(NPAIR - 1), None, ALU.min
                            ).then_inc(tables, 1)

            own.mark(v.tensor_scalar(part[:, 1:2], part[:, 0:1], R - 1, None, ALU.bitwise_and))
            own.settle()
            own.mark(v.tensor_copy(partf[:, :], part[:, 1:2]))
            own.settle()
            dve.wait_ge(batch_out, len(batches))

            def type_onehot(g, par, turn, quarters, first):
                dve.wait_ge(type_in[par], turn * 64 + 16 * quarters)
                if not first:
                    dve.wait_ge(coef_ps, g)
                v.tensor_scalar(onehot, types[par], partf[:, 0:1], None, ALU.is_equal).then_inc(oh_ok, 1)

            def coefficients(g, par, quarters, ms):
                dve.wait_ge(coef_ps, g + 1)
                to = coef[:, bass.ds(g * (GT * B), quarters * ms * B)].rearrange(
                    "p (q m b) -> p q m b", q=quarters, b=B)
                w = wT[:, bass.ds(g * GT, quarters * ms)].rearrange("p (q m o) -> p q m o", q=quarters, o=1)
                of = bank[par][:, :].rearrange("p (m q b) -> p q m b", q=4, b=B)[:, 0:quarters, 0:ms, :]
                v.tensor_tensor(to, of, w.to_broadcast([P, quarters, ms, B]), ALU.mult).then_inc(coef_ok, 1)

            type_onehot(0, 0, 0, 4, True)
            coefficients(0, 0, 4, GM)
            type_onehot(1, 1, 0, 4, False)
            coefficients(1, 1, 4, GM)
            with dve.Fori(1, NGRP // 2 - 1) as i:
                for par in range(2):
                    type_onehot(i * 2 + par, par, i, 4, False)
                    coefficients(i * 2 + par, par, 4, GM)
            type_onehot(NGRP - 2, 0, NGRP // 2 - 1, 4, False)
            coefficients(NGRP - 2, 0, 4, GM)
            type_onehot(NGRP - 1, 1, NGRP // 2 - 1, 1, False)
            rest = NTILE - (NGRP - 1) * GT
            assert rest <= GM
            coefficients(NGRP - 1, 1, 1, rest)

            own.mark(v.memset(ps_slot[:, :], 0.0))
            own.mark(v.memset(count[:, :], 0.0))
            own.mark(v.tensor_copy(token[:, :], part[:, 0:1]))
            dve.wait_ge(small_in, 96)
            dve.wait_ge(coef_ok, NGRP)
            own.settle()

            def build(j, lo, hi):
                window = nodes[:, bass.ds(j * WIN, WIN)].rearrange("p (o n) -> p o n", o=1).to_broadcast([P, B, WIN])
                with dve.Fori(lo, hi + 1) as m:
                    for u in range(2):
                        dve.wait_ge(S_used[u], m + j + 1)
                        c = coef[:, bass.ds(m * (2 * B) + u * B, B)].rearrange("p (b o) -> p b o", o=1)
                        v.scalar_tensor_tensor(
                            S[:, u, :].rearrange("p (b n) -> p b n", n=WIN), window,
                            dstT[:, bass.ds(m * 2 + u, 1)], c.to_broadcast([P, B, WIN]),
                            ALU.is_equal, ALU.mult).then_inc(S_ok[u], 1)

            def node_work(jj, r):
                if jj == 2:
                    dve.wait_ge(xf_ok, r + 1)
                    dve.wait_ge(xt_in, r * 16 + 16)
                    dve.wait_ge(x1_out, r * 16 + 16)
                    v.scalar_tensor_tensor(x1[:, :], ps_node[:, 0:D], 0.0, xt[:, :], ALU.max, ALU.add
                                           ).then_inc(x1_ok, 1)
                    dve.wait_ge(x1_ok, r + 2)
                    own.mark(v.bn_stats(bst[:, :], x1[:, :]))
                    own.settle_apart((tables, 2))
                    own.mark(v.bn_aggr(bmv[:, :], bst[:, :]))
                    own.settle()
                    v.tensor_scalar(brs[:, 0:1], bmv[:, 1:2], EPS, None, ALU.add).then_inc(sd_ok, 1)
                if jj == 3:
                    dve.wait_ge(sd_ok, r * 2 + 2)
                    own.mark(v.reciprocal(brs[:, 1:2], brs[:, 1:2]))
                    own.settle()
                    dve.wait_ge(xn_out, r * 16 + 16)
                    v.tensor_scalar(xn[:, :], x1[:, :], bmv[:, 0:1], brs[:, 1:2], ALU.subtract, ALU.mult
                                    ).then_inc(xn_ok, 1)
                if jj == 5:
                    dve.wait_ge(gate_ps, r + 1)
                    own.mark(v.tensor_tensor(gate[:, 0, :], ps_small[:, D:D + NE], bg_sb[:, :], ALU.add))
                    own.settle_apart((tables, 2))
                    own.mark(v.max(gate[:, 1, :], gate[:, 0, :]))
                    own.settle_apart((tables, 2))
                    own.mark(v.max_index(top[:, :], gate[:, 1, :], gate[:, 0, :]))
                    own.settle()
                    own.mark(v.tensor_copy(topf[:, :], top[:, 0:2]))
                    own.settle()
                    for c in range(2):
                        own.mark(v.tensor_scalar(pick[:, c, :], nodes[:, 0:NE], topf[:, c:c + 1], None, ALU.is_equal))
                    own.settle()
                    v.tensor_tensor(pick[:, 2, :], pick[:, 0, :], pick[:, 1, :], ALU.add).then_inc(pick_ok, 1)
                if jj == 6:
                    dve.wait_ge(rank_ps, r + 1)
                    own.mark(v.tensor_tensor(place[:, :], ps_small[:, 272:272 + NE], count[:, :], ALU.add))
                    own.settle()
                    own.mark(v.tensor_tensor(count[:, :], ps_small[:, 288:288 + NE], count[:, :], ALU.add))
                    for c in range(2):
                        own.mark(v.tensor_tensor_reduce(scr[:, :], place[:, :], pick[:, c, :], 1.0, 0.0,
                                                        ALU.mult, ALU.add, rank[:, c:c + 1]))
                        own.settle()
                    own.mark(v.tensor_copy(rank_i[:, 0, :], rank[:, :]))
                    own.settle()
                    own.mark(v.tensor_scalar(rank_i[:, 1, :], rank_i[:, 0, :], P - 1, None, ALU.bitwise_and))
                    own.mark(v.tensor_scalar(rank_i[:, 2, :], rank_i[:, 0, :], 7, None, ALU.arith_shift_right))
                    own.settle()
                    own.mark(v.tensor_copy(rank_f[:, 0, :], rank_i[:, 1, :]))
                    own.mark(v.scalar_tensor_tensor(rank_f[:, 1, :], topf[:, :], float(PER_E), rank_i[:, 2, :],
                                                    ALU.mult, ALU.add))
                    own.mark(v.tensor_scalar(token[:, :], token[:, :], 1.0, None, ALU.add))
                    own.settle()
                    dve.wait_ge(map_ok, r + 1)
                    for c in range(2):
                        own.mark(v.tensor_scalar(slot_oh[:, c, :], nodes[:, 0:P], rank_f[:, 0, c:c + 1], None,
                                                 ALU.is_equal))
                        own.mark(v.tensor_scalar(col_id[:, c, :], nodes[:, 0:NSLOT], rank_f[:, 1, c:c + 1],
                                                 token[:, 0:1], ALU.is_equal, ALU.mult))
                    own.settle()
                    v.tensor_scalar(token[:, :], token[:, :], float(P - 1), None, ALU.add).then_inc(oh2_ok, 1)
                    dve.wait_ge(oh2_ok, r + 1)

            MARKS = 23

            def tile(i, first):
                lo = dve.value_load(Mt[0:1, bass.ds(i * BPT, 1)], min_val=0, max_val=NPAIR - 1)
                for jj in range(BPT):
                    j = i * BPT + jj
                    hi = dve.value_load(Mt[0:1, bass.ds(j + 1, 1)], min_val=0, max_val=NPAIR - 1)
                    build(j, lo, hi)
                    lo = hi
                    if not first:
                        node_work(jj, i - 1)

            dve.wait_ge(tables, 2)
            dve.sem_inc(x1_ok, 1)
            tile(0, True)
            with dve.Fori(1, NT) as i:
                own.enter(i - 1, MARKS)
                tile(i, False)
                own.leave(NT - 1)
            for jj in range(BPT):
                node_work(jj, NT - 1)

            dve.wait_ge(map_ok, NT + 1)
            own.mark(v.memset(slot_f[:, :, :], 0.0))
            own.settle()
            own.mark(v.tensor_scalar(slot_f[:, 0, 0:NSLOT], ps_slot[:, 0:NSLOT], -1.0, 0.0, ALU.add, ALU.max))
            own.mark(v.tensor_scalar(slot_f[:, 1, 0:NSLOT], ps_slot[:, 0:NSLOT], 0.0, None, ALU.is_equal))
            own.mark(v.memset(slot_f[:, 1, NSLOT:], 1.0))
            own.settle()
            own.mark(v.tensor_copy(slot_i[:, :, 0], slot_f[:, 0, :]))
            own.mark(v.scalar_tensor_tensor(slot_i[:, :, 1], slot_f[:, 1, :], float(SKIP), slot_f[:, 0, :],
                                            ALU.mult, ALU.add))
            own.mark(v.tensor_scalar(nb[:, 0, :], count[:, :], float(P - 1), None, ALU.add))
            own.settle()
            own.mark(v.tensor_copy(nb_i[:, :], nb[:, 0, :]))
            own.settle()
            own.mark(v.tensor_scalar(nb_i[:, :], nb_i[:, :], 7, None, ALU.arith_shift_right))
            own.settle()
            own.mark(v.tensor_copy(nb[:, 0, :], nb_i[:, :]))
            own.settle()
            own.mark(v.tensor_scalar(nb[:, 2, :], nb[:, 0, :], -1.0, float(PER_E), ALU.mult, ALU.add))
            own.mark(v.tensor_copy(nb[:, 1, 0:1], nb[:, 0, 0:1]))
            own.settle()
            for e in range(1, NE):
                own.mark(v.tensor_tensor(nb[:, 1, e:e + 1], nb[:, 1, e - 1:e], nb[:, 0, e:e + 1], ALU.add))
                own.settle()
            own.mark(v.memset(blkrow[:, 0, :], 0.0))
            own.mark(v.tensor_copy(blkrow[:, 1, :], nodes[:, 0:NFFN]))
            own.settle()
            for e in range(NE):
                own.mark(v.tensor_scalar(blkrow[:, 2, :], nodes[:, 0:NFFN], nb[:, 1, e:e + 1], None, ALU.is_ge))
                own.settle()
                own.mark(v.tensor_tensor(blkrow[:, 0, :], blkrow[:, 0, :], blkrow[:, 2, :], ALU.add))
                own.mark(v.scalar_tensor_tensor(blkrow[:, 1, :], blkrow[:, 2, :], nb[:, 2, e:e + 1],
                                                blkrow[:, 1, :], ALU.mult, ALU.add))
                own.settle()
            own.mark(v.tensor_scalar(blk_e[0:1, :], blkrow[0:1, 0, :], float(NE - 1), None, ALU.min))
            own.settle()
            v.tensor_copy(blk_c[0:1, :], blkrow[0:1, 1, :]).then_inc(slots_ok, 1)
            dve.wait_ge(slots_ok, 1)
            dve.wait_ge(b_in, 32)

            def add_b1(k, e):
                dve.wait_ge(hid_ps, k + 1)
                if not (isinstance(k, int) and k == 0):
                    dve.wait_ge(act_ok, k)
                v.tensor_tensor(hid, bank[0][:, 0:H], b1_bc[:, bass.ds(e * H, H)], ALU.add).then_inc(hid_ok, 1)

            def add_b2(k, par, e):
                dve.wait_ge(y_ps, k + 1)
                if not (isinstance(k, int) and k < 2):
                    dve.wait_ge(y_out, k * 16 - 16)
                v.tensor_tensor(y_sb[par], bank[1][:, 0:D], b2_bc[:, bass.ds(e * D, D)], ALU.add).then_inc(y_ok, 1)

            def expert(k):
                return dve.value_load(blk_e[0:1, bass.ds(k, 1)], min_val=0, max_val=NE - 1)

            def turn_of(k, par):
                add_b1(k + 1, expert(k + 1))
                add_b2(k, par, expert(k))

            add_b1(0, expert(0))
            turn_of(0, 0)
            turn_of(1, 1)
            with dve.Fori(1, NFFN // 2 - 1) as i:
                for par in range(2):
                    turn_of(i * 2 + par, par)
            turn_of(NFFN - 2, 0)
            add_b2(NFFN - 1, 1, expert(NFFN - 1))


_INS = ['x', 'src', 'dst', 'edge_type_32', 'edge_weight1', 'L0_gnn_bases', 'L0_gnn_w_comp', 'L0_ffn_Wg',
        'L0_ffn_bg', 'L0_ffn_W1', 'L0_ffn_b1', 'L0_ffn_W2', 'L0_ffn_b2']


def kernel(**inputs):
    import numpy as _np
    import concourse.bacc as _bacc
    from concourse.bass_utils import run_bass_kernel_spmd as _run

    nc = _bacc.Bacc("TRN2", target_bir_lowering=False, num_devices=1)
    arrays, args = {}, []
    for name in _INS:
        a = _np.ascontiguousarray(inputs[name])
        arrays[f"in_{name}"] = a
        args.append(nc.dram_tensor(f"in_{name}", a.shape, mybir.dt.from_np(a.dtype), kind="ExternalInput").ap())
    out = nc.dram_tensor("out_rows", inputs["x"].shape, F32, kind="ExternalOutput").ap()
    gnn_moe_layer(nc, *args, out)
    r = _run(nc, [arrays], core_ids=[0])
    return r.results[0]["out_rows"]
```

```python
from contextlib import ExitStack

import concourse.bass as bass
from concourse import mybir

P = 128
ALU = mybir.AluOpType
AX = mybir.AxisListType
ACT = mybir.ActivationFunctionType
F32 = mybir.dt.float32
I32 = mybir.dt.int32
U32 = mybir.dt.uint32
U16 = mybir.dt.uint16
BF16 = mybir.dt.bfloat16

EPS = 1e-5
WIN = 16
RING = 8
STEP = 6
CODE = 2048
ROUND = 1.5 * (1 << 23)
LAG = 4
SKIP = 1 << 24


def wait_apart(eng, sem, value, passed_by):
    value = value if isinstance(value, int) else eng.to_reg(value)
    eng.wait_ge(*passed_by)
    eng.wait_ge(sem, value)


class Tally:

    def __init__(self, eng, sem):
        self.eng, self.sem, self.base, self.n = eng, sem, 0, 0

    def mark(self, ins):
        ins.then_inc(self.sem, 1)
        self.n += 1

    def settle(self):
        self.eng.wait_ge(self.sem, self.base + self.n)

    def settle_apart(self, passed_by):
        wait_apart(self.eng, self.sem, self.base + self.n, passed_by)

    def enter(self, turn, per):
        self.start, self.per = self.base + self.n, per
        self.base, self.n = self.start + turn * per, 0

    def leave(self, turns):
        assert self.n == self.per, (self.n, self.per)
        self.base, self.n = self.start + turns * self.per, 0


def gnn_moe_layer(nc, x, src, dst, etype, eweight, bases, w_comp, Wg, bg, W1, b1, W2, b2, out):
    N, D = x.shape
    E = src.shape[0]
    B = bases.shape[0]
    R = w_comp.shape[0]
    NE, _, H = W1.shape
    NT = -(-N // P)
    LAST = N - (NT - 1) * P
    BPT = P // WIN
    NBLK = NT * BPT
    EPAIR = 2 * P
    NPAIR = -(-E // EPAIR)
    NTILE = 2 * NPAIR
    NB1 = NBLK + 2
    JC = NBLK // 4
    QMAX = NBLK + (NTILE + NBLK) // STEP + 1
    NCOL = -(-NTILE // P)
    DH = D // P
    HC = H // P
    GT = 64
    GM = GT // 4
    NGRP = -(-NTILE // GT)
    PER_E = -(-N // P)
    NSLOT = NE * PER_E
    NFFN = (2 * N + NE * (P - 1)) // P
    NFFN += NFFN % 2
    NSLOT_PAD = NSLOT + NFFN - (2 * N) // P + 1
    NSLOT_PAD += -NSLOT_PAD % 8
    assert D == 256 and B * WIN == P and R * 4 == P and NE == 8 and NSLOT_PAD <= 512 and E < 1 << 24

    h_dram = nc.dram_tensor("h_scratch", (N, D), F32, kind="Internal").ap()
    xn_dram = nc.dram_tensor("xn_scratch", (N, D), F32, kind="Internal").ap()

    with ExitStack() as ctx:
        def sb(name, shape, dt=F32):
            return ctx.enter_context(nc.sbuf_tensor(name, shape, dt))

        def sem(name):
            return ctx.enter_context(nc.semaphore(name))

        bank = [ctx.enter_context(nc.psum_tensor(f"bank{n}", [P, 512], F32)) for n in range(8)]
        acc, tr = bank[0:2], bank[2:4]
        ps_node, ps_small, ps_slot = bank[4], bank[5], bank[6]

        bases_sb = sb("bases_sb", [P, B, DH, D])
        ffn_w = sb("ffn_w", [P, NE * DH * H + NE * HC * D])
        w1_sb = ffn_w[:, 0:NE * DH * H]
        w2_sb = ffn_w[:, NE * DH * H:]
        xin = ffn_w[:, 0:NT * D].rearrange("p (t d) -> p t d", d=D)
        ONEHOT0 = NT * D
        onehot = ffn_w[:, ONEHOT0:ONEHOT0 + GM * P]
        WT0 = ONEHOT0 + GM * P
        wT = ffn_w[:, WT0:WT0 + NCOL * P]
        assert WT0 + NCOL * P <= NE * DH * H + NE * HC * D
        RING0 = NE * DH * H
        ring = ffn_w[:, RING0:RING0 + RING * 2 * D]
        assert RING0 + RING * 2 * D <= ONEHOT0

        coef = sb("coef", [P, (NTILE + STEP) * B])
        RAW = NCOL * P
        raw_i = [coef[:, k * RAW:(k + 1) * RAW].bitcast(I32) for k in range(2)]
        raw_f = [coef[:, k * RAW:(k + 1) * RAW] for k in range(2, 5)]
        passed = coef[:, 5 * RAW:5 * RAW + NCOL * NB1 // 2].bitcast(BF16).rearrange("p (c j) -> p c j", j=NB1)
        BELOW0 = 5 * RAW + NCOL * NB1 // 2
        below = coef[0:JC, BELOW0:BELOW0 + 4 * NB1].rearrange("p (c j) -> p c j", j=NB1)
        assert BELOW0 + 4 * NB1 <= NTILE * B
        used = [0]

        def late(n):
            used[0] += n
            assert used[0] <= NTILE * B
            return coef[:, used[0] - n:used[0]]

        b1_bc, b2_bc = late(NE * H), late(NE * D)
        hid, act, actT, xbT = late(H), late(H), late(H), late(D)
        slot_f = late(2 * NSLOT_PAD).rearrange("p (o c) -> p o c", o=2)
        slot_i = late(2 * NSLOT_PAD).bitcast(I32).rearrange("p (c o) -> p c o", o=2)
        y_sb, xb = [late(D), late(D)], [late(D), late(D)]

        dstT = sb("dstT", [P, NCOL * P])
        srcT = sb("srcT", [P, NCOL * P], I32)
        nodes = sb("nodes", [P, NBLK * WIN], U16)
        S = sb("S", [P, 2 * STEP, P])
        blk = sb("blk", [P, 2, D])
        aggT = sb("aggT", [P, DH * B * P])
        pick_scr = aggT[:, 0:5 * NB1]
        bases_flat = bases_sb[:, :, :, :].rearrange("p b h o -> p (b h o)")
        types = [bases_flat[:, n * GM * P:(n + 1) * GM * P].bitcast(I32) for n in range(2)]
        idx = sb("idx", [P, 2, 2 * RING], I32)
        ident = sb("ident", [P, P])
        lower = sb("lower", [P, P])
        ones = sb("ones", [P, P])
        zeros = sb("zeros", [P, D])
        comp4 = sb("comp4", [P, 4 * B])
        part = sb("part", [P, 2], I32)
        partf = sb("partf", [P, 1])
        end_i = sb("end_i", [P, NCOL], I32)
        end_b = sb("end_b", [P, NCOL])
        tile_id = sb("tile_id", [P, NCOL])
        block_id = sb("block_id", [P, 4])
        steps_of = sb("steps_of", [JC, 4])
        offset = pick_scr[:, 0:NB1]
        first_tile, first_row = pick_scr[:, NB1:2 * NB1], pick_scr[0:1, 2 * NB1:3 * NB1]
        ends_of = sb("ends_of", [JC, 2, 4])
        div_f = sb("div_f", [P, 3, NCOL])
        div_i = sb("div_i", [P, NCOL], I32)
        last_step = sb("last_step", [P, NCOL])
        block_tab = sb("block_tab", [1, NB1], I32)
        free_at = sb("free_at", [1, NCOL * P // 2], I32)
        ones16 = sb("ones16", [P, P], BF16)
        stats = sb("stats", [P, 8, 6])
        mv = sb("mv", [P, NT, 2])
        mv7 = sb("mv7", [P, 7, 2])
        rs = sb("rs", [P, NT])
        xt = sb("xt", [P, D])
        x1 = sb("x1", [P, D])
        xn = sb("xn", [P, D])
        xnT = sb("xnT", [P, D])
        bst = sb("bst", [P, 6])
        bmv = sb("bmv", [P, 2])
        brs = sb("brs", [P, 2])
        Wg_sb = sb("Wg_sb", [P, DH, NE])
        bg_sb = sb("bg_sb", [P, NE])
        gate = sb("gate", [P, 2, NE])
        top = sb("top", [P, NE], U32)
        pick = sb("pick", [P, 3, NE])
        count = sb("count", [P, NE])
        place = sb("place", [P, NE])
        picked = sb("picked", [P, 2, NE])
        slot = sb("slot", [P, 5, 2])
        eps = sb("eps", [P, 1])
        slot_oh = sb("slot_oh", [P, 2, P])
        col_id = sb("col_id", [P, 2, NSLOT])
        token = sb("token", [P, 2])
        nb = sb("nb", [P, 3, NE])
        nb_i = sb("nb_i", [P, NE], I32)
        blkrow = sb("blkrow", [P, 3, NFFN])
        blk_e = sb("blk_e", [1, NFFN], I32)
        blk_c = sb("blk_c", [1, NFFN], I32)
        gidx = sb("gidx", [P, 2, 2], I32)
        sidx = sb("sidx", [P, 2, 2], I32)

        pads = sem("pads")
        raw_in = [sem(f"raw_in{k}") for k in range(3)]
        x_in = sem("x_in")
        consts = sem("consts")
        small_in = sem("small_in")
        bases_in = sem("bases_in")
        conv = sem("conv")
        batch = sem("batch")
        batch_out = sem("batch_out")
        var_ok, std_ok, rs_ok = sem("var_ok"), sem("std_ok"), sem("rs_ok")
        norm_d, norm_p = sem("norm_d"), sem("norm_p")
        h_out = sem("h_out")
        passed_ok, first_ok = sem("passed_ok"), sem("first_ok")
        below_ok, Q_ok, last_ok, free_ps = sem("below_ok"), sem("Q_ok"), sem("last_ok"), sem("free_ps")
        tables = sem("tables")
        type_in = [sem("type_in0"), sem("type_in1")]
        oh_ok, oh_used, coef_ps, coef_ok = sem("oh_ok"), sem("oh_used"), sem("coef_ps"), sem("coef_ok")
        w_in, b_in = sem("w_in"), sem("b_in")
        idx_ok = sem("idx_ok")
        ring_in = [sem(f"ring_in{k}") for k in range(RING)]
        gathered = sem("gathered")
        released = sem("released")
        S_ok = [sem(f"S_ok{k}") for k in range(STEP // 2)]
        S_used = [sem(f"S_used{k}") for k in range(STEP // 2)]
        blk_ok = sem("blk_ok")
        acc_zero = sem("acc_zero")
        tr_ok, aggT_ok = sem("tr_ok"), sem("aggT_ok")
        xf_ok = sem("xf_ok")
        xt_in, x1_ok, x1_out = sem("xt_in"), sem("x1_ok"), sem("x1_out")
        var2_ok, sd_ok, xn_ok, xn_out = sem("var2_ok"), sem("sd_ok"), sem("xn_ok"), sem("xn_out")
        xnT_ps, xnT_ok, gate_ps = sem("xnT_ps"), sem("xnT_ok"), sem("gate_ps")
        pick_ok, rank_ps, oh2_ok, map_ok = sem("pick_ok"), sem("rank_ps"), sem("oh2_ok"), sem("map_ok")
        dve_own, act_own, pool_own = sem("dve_own"), sem("act_own"), sem("pool_own")
        slots_ok = sem("slots_ok")
        g_idx_ok, s_idx_ok = sem("g_idx_ok"), sem("s_idx_ok")
        xb_in = [sem("xb_in0"), sem("xb_in1")]
        xbT_ps, xbT_ok, hid_ps, hid_ok = sem("xbT_ps"), sem("xbT_ok"), sem("hid_ps"), sem("hid_ok")
        act_ok, actT_ps, actT_ok, y_ps, y_ok = (sem("act_ok"), sem("actT_ps"), sem("actT_ok"),
                                                sem("y_ps"), sem("y_ok"))
        y_out = sem("y_out")

        block = ctx.enter_context(nc.Block())

        e_full = (E // (P * P)) * P * P
        e_rows = (E - e_full) // P
        e_rest = E - e_full - e_rows * P
        lists = [src, dst, eweight.rearrange("e o -> (e o)")]
        raw_to = [raw_i[0], raw_i[1], raw_f[2]]
        raw_fl = [raw_f[0], raw_f[1], raw_f[2]]
        batches = [(k, c, min(4, NCOL - c)) for k in range(3) for c in range(0, NCOL, 4)]

        def block_entry(eng, j):
            entry = nc.values_load(block_tab[0:1, bass.ds(j, 1)], engines=[eng.engine], min_val=0,
                                   max_val=QMAX * CODE + NTILE,
                                   skip_runtime_bounds_check_because="it counts steps and tiles that exist")
            entry = eng.snap(entry & (CODE * CODE - 1))
            return eng.snap(entry // CODE), eng.snap(entry & (CODE - 1))

        def tile_of(eng, step, entry):
            return nc.s_assert_within(eng.snap(((step - entry[0]) * STEP + entry[1]) & (CODE - 1)), 0, NTILE - 1,
                                      skip_runtime_bounds_check_because="the last step begins at a tile that exists")

        def steps_of_tile(r):
            return LAST if isinstance(r, int) and r == NT - 1 else P

        @block.sync
        def _(sp):
            sp.wait_ge(pads, 4)
            for k in range(3):
                to = raw_to[k].rearrange("p (c e) -> p c e", e=P)
                c = e_full // (P * P)
                sp.dma_start(to[:, 0:c, :], lists[k][0:e_full].rearrange("(c p e) -> p c e", p=P, e=P)
                             ).then_inc(raw_in[k], 16)
                sp.dma_start(to[0:e_rows, c, :], lists[k][e_full:E - e_rest].rearrange("(p e) -> p e", e=P)
                             ).then_inc(raw_in[k], 16)
                sp.dma_start(to[e_rows:e_rows + 1, c, 0:e_rest],
                             lists[k][E - e_rest:E].rearrange("(o e) -> o e", o=1)).then_inc(raw_in[k], 16)
            full = (NT - 1) // 7 * 7
            for c in range(0, full, 7):
                sp.dma_start(xin[:, c:c + 7, :], x[c * P:(c + 7) * P, :].rearrange("(t p) d -> p t d", p=P)
                             ).then_inc(x_in, 16)
            sp.dma_start(xin[:, full:NT - 1, :],
                         x[full * P:(NT - 1) * P, :].rearrange("(t p) d -> p t d", p=P)).then_inc(x_in, 16)
            sp.dma_start(xin[0:LAST, NT - 1, :], x[(NT - 1) * P:N, :]).then_inc(x_in, 16)
            sp.wait_ge(consts, 7)
            for q in range(4):
                sp.dma_start(comp4[R * q:R * q + R, B * q:B * q + B], w_comp).then_inc(small_in, 16)
            sp.dma_start(Wg_sb[:, :, :], Wg.rearrange("(h p) e -> p h e", p=P)).then_inc(small_in, 16)
            sp.dma_start(bg_sb[:, :], bg.rearrange("(o e) -> o e", o=1).to_broadcast([P, NE])
                         ).then_inc(small_in, 16)
            sp.wait_ge(norm_p, NT - NT // 2)
            sp.wait_ge(norm_d, NT // 2)
            sp.dma_start(h_dram[0:(NT - 1) * P, :].rearrange("(t p) d -> p t d", p=P), xin[:, 0:NT - 1, :]
                         ).then_inc(h_out, 16)
            sp.dma_start(h_dram[(NT - 1) * P:N, :], xin[0:LAST, NT - 1, :]).then_inc(h_out, 16)

            def load_types(g, par, quarters, first):
                if not first:
                    sp.wait_ge(oh_ok, g - 1)
                for q in range(quarters):
                    n = min(GM * P, E - g * (GT * P) - q * GM * P) if isinstance(g, int) else GM * P
                    sp.dma_start(types[par][R * q:R * q + R, 0:n],
                                 etype[bass.ds(g * (GT * P) + q * GM * P, n)].rearrange("(o n) -> o n", o=1)
                                 .to_broadcast([R, n])).then_inc(type_in[par], 16)

            load_types(0, 0, 4, True)
            load_types(1, 1, 4, True)
            with sp.Fori(1, NGRP // 2 - 1) as i:
                for par in range(2):
                    load_types(i * 2 + par, par, 4, False)
            load_types(NGRP - 2, 0, 4, False)
            load_types(NGRP - 1, 1, 1, False)
            sp.wait_ge(oh_ok, NGRP)
            for b in range(B):
                sp.dma_start(bases_sb[:, b, :, :], bases[b].rearrange("(h p) o -> p h o", p=P)
                             ).then_inc(bases_in, 16)

            def relay(slot, turn, m, lagged):
                sp.wait_ge(ring_in[slot], turn * 32 + 32)
                sp.sem_inc(gathered, 2)
                if lagged:
                    at = sp.value_load(free_at[0:1, bass.ds(m - LAG, 1)], min_val=1, max_val=QMAX + 1)
                    sp.wait_ge(S_used[-1], at)
                    sp.sem_inc(released, 1)

            sp.wait_ge(tables, 5)
            for m in range(RING):
                relay(m, 0, m, m >= LAG)
            with sp.Fori(1, NPAIR // RING) as turn:
                for k in range(RING):
                    relay(k, turn, turn * RING + k, True)
            for k in range(NPAIR % RING):
                relay(k, NPAIR // RING, NPAIR // RING * RING + k, True)
            sp.sem_inc(gathered, STEP)

        @block.gpsimd
        def _(pool):
            g = nc.gpsimd
            for k, v in ((0, 0), (1, NBLK * WIN - 1)):
                g.memset(raw_i[k][:, (NCOL - 1) * P:], v).then_inc(pads, 1)
            g.memset(raw_f[2][:, (NCOL - 1) * P:], 0.0).then_inc(pads, 1)
            g.memset(xin[:, NT - 1, :], 0.0).then_inc(pads, 1)
            g.memset(ones[:, :], 1.0).then_inc(pool_own, 1)
            g.memset(zeros[:, :], 0.0).then_inc(consts, 1)
            g.memset(comp4[:, :], 0.0).then_inc(consts, 1)
            g.memset(eps[:, :], EPS).then_inc(consts, 1)
            g.iota(nodes[:, :], [[1, NBLK * WIN]], base=0, channel_multiplier=0).then_inc(consts, 1)
            g.iota(part[:, 0:1], [[0, 1]], base=0, channel_multiplier=1).then_inc(consts, 1)
            pool.wait_ge(pool_own, 1)
            g.affine_select(out=ident[:, :], in_=ones[:, :], compare_op=ALU.is_equal, fill=0.0, base=0,
                            pattern=[[-1, P]], channel_multiplier=1).then_inc(consts, 1)
            g.affine_select(out=lower[:, :], in_=ones[:, :], compare_op=ALU.is_gt, fill=0.0, base=0,
                            pattern=[[1, P]], channel_multiplier=-1).then_inc(consts, 1)
            pool.wait_ge(rs_ok, 1)
            for t in range(NT // 2, NT):
                g.tensor_scalar(xin[:, t, :], xin[:, t, :], mv[:, t, 0:1], rs[:, t:t + 1],
                                ALU.subtract, ALU.mult).then_inc(norm_p, 1)

            pool.wait_ge(batch_out, len([0 for k, _, _ in batches if k == 0]))
            pool.wait_ge(h_out, 32)
            turns = NPAIR // (2 * RING)

            def gathers(half, m0, n, copies, first):
                if not first:
                    pool.wait_ge(released, m0 - RING + 1)
                g.tensor_copy(idx[:, half, 0:2 * n], srcT[:, bass.ds(m0 * 2, 2 * n)]).then_inc(idx_ok, 1)
                wait_apart(pool, idx_ok, copies + 1, (h_out, 32))
                for k in range(n):
                    if not first:
                        wait_apart(pool, released, m0 + k - RING + 1, (h_out, 32))
                    for t in range(2):
                        at = (k * 2 + t) * D
                        g.indirect_dma_start(
                            out=ring[:, at:at + D], out_offset=None, in_=h_dram,
                            in_offset=bass.IndirectOffsetOnAxis(ap=idx[:, half, 2 * k + t:2 * k + t + 1], axis=0)
                        ).then_inc(ring_in[k], 16)

            gathers(0, 0, RING, 0, True)
            gathers(1, RING, RING, 1, False)
            with pool.Fori(1, turns) as turn:
                gathers(0, turn * 2 * RING, RING, turn * 2, False)
                gathers(1, turn * 2 * RING + RING, RING, turn * 2 + 1, False)
            rest = NPAIR - turns * 2 * RING
            assert 0 < rest <= RING
            gathers(0, turns * 2 * RING, rest, turns * 2, False)

            pool.wait_ge(slots_ok, 1)
            pool.wait_ge(xn_out, 16 * NT + 16)
            pool.wait_ge(x1_out, 16 * NT + 16)
            pool.wait_ge(w_in, 16 * 2 * NE)

            def fetch(k, par):
                c = pool.value_load(blk_c[0:1, bass.ds(k, 1)], min_val=0, max_val=NSLOT_PAD - 1)
                g.tensor_copy(gidx[:, par, :], slot_i[:, bass.ds(c, 1), :].rearrange("p a b -> p (a b)")
                              ).then_inc(g_idx_ok, 1)
                wait_apart(pool, g_idx_ok, k + 1, (slots_ok, 1))
                g.indirect_dma_start(
                    out=xb[par], out_offset=None, in_=xn_dram,
                    in_offset=bass.IndirectOffsetOnAxis(ap=gidx[:, par, 0:1], axis=0)).then_inc(xb_in[par], 16)

            def add_rows(k, par):
                c = pool.value_load(blk_c[0:1, bass.ds(k, 1)], min_val=0, max_val=NSLOT_PAD - 1)
                g.tensor_copy(sidx[:, par, :], slot_i[:, bass.ds(c, 1), :].rearrange("p a b -> p (a b)")
                              ).then_inc(s_idx_ok, 1)
                pool.wait_ge(s_idx_ok, k + 1)
                pool.wait_ge(y_ok, k + 1)
                if not (isinstance(k, int) and k == 0):
                    wait_apart(pool, y_out, k * 16, (slots_ok, 1))
                g.indirect_dma_start(
                    out=out, out_offset=bass.IndirectOffsetOnAxis(ap=sidx[:, par, 1:2], axis=0),
                    in_=y_sb[par], in_offset=None, bounds_check=N - 1, oob_is_err=False,
                    compute_op=ALU.add).then_inc(y_out, 16)

            fetch(0, 0)
            fetch(1, 1)

            def turn_of(k, par, first, last):
                if not last:
                    pool.wait_ge(xbT_ps, k + 1)
                    fetch(k + 2, par)
                add_rows(k, par)

            turn_of(0, 0, True, False)
            turn_of(1, 1, True, False)
            with pool.Fori(1, NFFN // 2 - 1) as t:
                for par in range(2):
                    turn_of(t * 2 + par, par, False, False)
            for par in range(2):
                turn_of(NFFN - 2 + par, par, False, True)
            pool.wait_ge(y_out, NFFN * 16)

        @block.tensor
        def _(pe):
            t = nc.tensor
            pe.wait_ge(consts, 7)
            for n, (k, c, w) in enumerate(batches):
                if c == 0:
                    if k < 2:
                        pe.wait_ge(conv, k + 1)
                    else:
                        pe.wait_ge(raw_in[2], 48)
                if n >= 8:
                    pe.wait_ge(batch_out, n - 7)
                for u in range(w):
                    mm = t.transpose(bank[n % 8][:, u * P:(u + 1) * P],
                                     raw_fl[k][:, (c + u) * P:(c + u + 1) * P], ident[:, :])
                mm.then_inc(batch, 1)
            pe.wait_ge(passed_ok, NCOL + 1)
            pe.wait_ge(batch_out, len(batches))
            for c in range(NCOL):
                t.matmul(bank[4][:, 0:NB1], ones16[:, :], passed[:, c, :], start=(c == 0), stop=(c == NCOL - 1))
            for n in range(8):
                k, nxt = n % 4, n // 4
                for c in range(NCOL):
                    mm = t.matmul(bank[5][0:JC, n:n + 1], passed[:, c, k * JC + nxt:(k + 1) * JC + nxt],
                                  ones16[:, 0:1], start=(c == 0), stop=(c == NCOL - 1))
            mm.then_inc(first_ok, 1)
            pe.wait_ge(below_ok, 4)
            for k in range(4):
                mm = t.matmul(bank[6][:, 0:NB1], ones[0:JC, :], below[:, k, :], start=(k == 0), stop=(k == 3))
            mm.then_inc(Q_ok, 1)
            pe.wait_ge(last_ok, 1)
            for c in range(NCOL):
                mm = t.matmul(bank[c // 4][0:1, c % 4 * P:(c % 4 + 1) * P], last_step[:, c:c + 1], ident[:, :],
                              start=True, stop=True)
            mm.then_inc(free_ps, 1)
            pe.wait_ge(small_in, 96)

            def comps(g, par, first):
                pe.wait_ge(oh_ok, g + 1)
                if not first:
                    pe.wait_ge(coef_ok, g - 1)
                for m in range(GM):
                    mm = t.matmul(bank[par][:, m * 4 * B:(m + 1) * 4 * B], onehot[:, m * P:(m + 1) * P],
                                  comp4[:, :], start=True, stop=True)
                mm.then_inc(coef_ps, 1)

            comps(0, 0, True)
            comps(1, 1, True)
            with pe.Fori(1, NGRP // 2) as i:
                for par in range(2):
                    comps(i * 2 + par, par, False)
            assert NGRP % 2 == 0

            pe.wait_ge(bases_in, 16 * B)
            pe.wait_ge(coef_ok, NGRP)
            for used in S_used:
                t.matmul(ps_small[:, 0:NE], ones[:, :], ones[:, 0:NE], start=True, stop=True).then_inc(used, 1)
            pe.wait_ge(tables, 5)

            def steps(j, jj, entry, following):
                wait_apart(pe, acc_zero, j + 1, (tables, 5))
                with pe.Fori(entry[0], following[0]) as g:
                    first = tile_of(pe, g, entry)
                    pe.wait_ge(gathered, first + STEP)
                    for u in range(STEP):
                        if u % 2 == 0:
                            pe.wait_ge(S_ok[u // 2], g + 1)
                        mm = t.matmul(acc[jj % 2][:, 0:D], S[:, jj % 2 * STEP + u, :],
                                      ring[:, bass.ds((first + u) % (2 * RING) * D, D)],
                                      start=False, stop=False, skip_group_check=True)
                        if u % 2 == 1:
                            mm.then_inc(S_used[u // 2], 1)

            def turn_block(j, par):
                pe.wait_ge(blk_ok, j + 1)
                pe.wait_ge(aggT_ok, j + 1)
                for h in range(DH):
                    mm = t.transpose(tr[par][:, h * P:(h + 1) * P], blk[:, par, h * P:(h + 1) * P], ident[:, :])
                mm.then_inc(tr_ok, 1)

            def transform(r):
                pe.wait_ge(aggT_ok, r * BPT + BPT + 2)
                pe.wait_ge(x1_ok, r + 1)
                for n in range(B * DH):
                    b, h = n // DH, n % DH
                    mm = t.matmul(ps_node[:, 0:D], aggT[:, (h * B + b) * P:(h * B + b + 1) * P],
                                  bases_sb[:, b, h, :], start=(n == 0), stop=(n == B * DH - 1))
                mm.then_inc(xf_ok, 1)

            def norm_work(jj, r):
                if jj == 5:
                    pe.wait_ge(xn_ok, r + 1)
                    for h in range(DH):
                        mm = t.transpose(ps_small[:, h * P:(h + 1) * P], xn[:, h * P:(h + 1) * P], ident[:, :])
                    mm.then_inc(xnT_ps, 1)
                if jj == 6:
                    pe.wait_ge(xnT_ok, r + 1)
                    for h in range(DH):
                        mm = t.matmul(ps_small[:, D:D + NE], xnT[:, h * P:(h + 1) * P], Wg_sb[:, h, :],
                                      start=(h == 0), stop=(h == DH - 1))
                    mm.then_inc(gate_ps, 1)

            def route_work(jj, r):
                if jj == 2:
                    k = steps_of_tile(r)
                    pe.wait_ge(pick_ok, r + 1)
                    t.matmul(ps_small[:, 272:272 + NE], lower[0:k, :], pick[0:k, 2, :], start=True, stop=True)
                    t.matmul(ps_small[:, 288:288 + NE], ones[0:k, :], pick[0:k, 2, :], start=True, stop=True
                             ).then_inc(rank_ps, 1)
                if jj == 7:
                    k = steps_of_tile(r)
                    pe.wait_ge(oh2_ok, r + 1)
                    for c in range(2):
                        mm = t.matmul(ps_slot[:, 0:NSLOT], slot_oh[0:k, c, :], col_id[0:k, c, :],
                                      start=False, stop=False, skip_group_check=True)
                    mm.then_inc(map_ok, 1)

            def tile(i, first):
                entry = block_entry(pe, i * BPT)
                for jj in range(BPT):
                    j = i * BPT + jj
                    following = block_entry(pe, j + 1)
                    steps(j, jj, entry, following)
                    entry = following
                    if jj == 1 and not first:
                        transform(i - 1)
                    if not (first and jj == 0):
                        turn_block(j - 1, (jj - 1) % 2)
                    if not first:
                        norm_work(jj, i - 1)
                    if not (isinstance(i, int) and i < 2):
                        route_work(jj, i - 2)

            pe.sem_inc(map_ok, 1)
            tile(0, True)
            tile(1, False)
            with pe.Fori(2, NT) as i:
                tile(i, False)
            turn_block(NBLK - 1, 1)
            transform(NT - 1)
            for jj in range(BPT):
                norm_work(jj, NT - 1)
                route_work(jj, NT - 2)
            for jj in range(BPT):
                route_work(jj, NT - 1)

            pe.wait_ge(slots_ok, 1)
            pe.wait_ge(w_in, 16 * 2 * NE)
            pe.wait_ge(acc_zero, NBLK + 2)
            ps_h, ps_y, ps_xT, ps_aT = bank[0], bank[1], bank[2], bank[3]

            def rows_T(k, par, turn):
                pe.wait_ge(xb_in[par], turn * 16 + 16)
                if not (isinstance(k, int) and k == 0):
                    pe.wait_ge(xbT_ok, k)
                for h in range(DH):
                    mm = t.transpose(ps_xT[:, h * P:(h + 1) * P], xb[par][:, h * P:(h + 1) * P], ident[:, :])
                mm.then_inc(xbT_ps, 1)

            def expert(k):
                return pe.value_load(blk_e[0:1, bass.ds(k, 1)], min_val=0, max_val=NE - 1)

            def up(k, e):
                pe.wait_ge(xbT_ok, k + 1)
                if not (isinstance(k, int) and k == 0):
                    pe.wait_ge(hid_ok, k)
                for h in range(DH):
                    mm = t.matmul(ps_h[:, 0:H], xbT[:, h * P:(h + 1) * P],
                                  w1_sb[:, bass.ds(e * (DH * H) + h * H, H)], start=(h == 0), stop=(h == DH - 1))
                mm.then_inc(hid_ps, 1)

            def hidden_T(k):
                pe.wait_ge(act_ok, k + 1)
                if not (isinstance(k, int) and k == 0):
                    pe.wait_ge(actT_ok, k)
                for c in range(HC):
                    mm = t.transpose(ps_aT[:, c * P:(c + 1) * P], act[:, c * P:(c + 1) * P], ident[:, :])
                mm.then_inc(actT_ps, 1)

            def down(k, e):
                pe.wait_ge(actT_ok, k + 1)
                if not (isinstance(k, int) and k == 0):
                    pe.wait_ge(y_ok, k)
                for c in range(HC):
                    mm = t.matmul(ps_y[:, 0:D], actT[:, c * P:(c + 1) * P],
                                  w2_sb[:, bass.ds(e * (HC * D) + c * D, D)], start=(c == 0), stop=(c == HC - 1))
                mm.then_inc(y_ps, 1)

            def turn_of(k, par, turn, ahead):
                e = expert(k)
                hidden_T(k)
                if ahead >= 1:
                    up(k + 1, expert(k + 1))
                if ahead >= 2:
                    rows_T(k + 2, par, turn + 1)
                down(k, e)

            rows_T(0, 0, 0)
            up(0, expert(0))
            rows_T(1, 1, 0)
            turn_of(0, 0, 0, 2)
            turn_of(1, 1, 0, 2)
            with pe.Fori(1, NFFN // 2 - 1) as i:
                for par in range(2):
                    turn_of(i * 2 + par, par, i, 2)
            turn_of(NFFN - 2, 0, NFFN // 2 - 1, 1)
            turn_of(NFFN - 1, 1, NFFN // 2 - 1, 0)

        @block.scalar
        def _(act_):
            a = nc.scalar
            for n, (k, c, w) in enumerate(batches):
                act_.wait_ge(batch, n + 1)
                to = (srcT, dstT, wT)[k][:, c * P:(c + w) * P]
                a.activation(to, bank[n % 8][:, 0:w * P], ACT.Copy).then_inc(batch_out, 1)
            act_.wait_ge(var_ok, 1)
            a.activation(rs[:, :], mv[:, :, 1], ACT.Sqrt).then_inc(std_ok, 1)
            act_.wait_ge(h_out, 32)
            act_.wait_ge(coef_ok, NGRP)
            for e in range(NE):
                act_.dma_start(w1_sb[:, e * DH * H:(e + 1) * DH * H].rearrange("p (h n) -> p h n", n=H),
                               W1[e].rearrange("(h p) n -> p h n", p=P)).then_inc(w_in, 16)
            act_.wait_ge(consts, 7)
            for n in range(2):
                a.activation(acc[n][:, 0:D], zeros[:, :], ACT.Copy).then_inc(acc_zero, 1)
            act_.wait_ge(tables, 5)

            def block_out(j, jj, following):
                act_.wait_ge(S_used[-1], following[0] + 1)
                if not (isinstance(j, int) and j < 2):
                    act_.wait_ge(tr_ok, j - 1)
                a.activation(blk[:, jj % 2, :], acc[jj % 2][:, 0:D], ACT.Copy).then_inc(blk_ok, 1)
                act_.wait_ge(blk_ok, j + 1)
                a.activation(acc[jj % 2][:, 0:D], zeros[:, :], ACT.Copy).then_inc(acc_zero, 1)

            def block_T(j, jj, prev):
                act_.wait_ge(tr_ok, j + 1)
                if jj == 0 and prev is not None:
                    act_.wait_ge(xf_ok, prev + 1)
                to = aggT[:, :].rearrange("p (g n) -> p g n", n=P)[:, :, jj * WIN:(jj + 1) * WIN]
                a.activation(to, tr[jj % 2][:, 0:D].rearrange("p (g n) -> p g n", n=WIN), ACT.Copy
                             ).then_inc(aggT_ok, 1)

            def norm_work(jj, r):
                k = steps_of_tile(r)
                rows = bass.ds(r * P, k)
                if jj == 0:
                    act_.wait_ge(x1_ok, r + 1)
                    act_.dma_start(xt[0:k, :], x[rows, :]).then_inc(xt_in, 16)
                if jj == 2:
                    act_.wait_ge(x1_ok, r + 2)
                    act_.dma_start(out[rows, :], x1[0:k, :]).then_inc(x1_out, 16)
                if jj == 3:
                    act_.wait_ge(var2_ok, r + 1)
                    a.activation(brs[:, 0:1], bmv[:, 1:2], ACT.Sqrt, bias=eps[:, 0:1]).then_inc(sd_ok, 1)
                if jj == 5:
                    act_.wait_ge(xn_ok, r + 1)
                    act_.dma_start(xn_dram[rows, :], xn[0:k, :]).then_inc(xn_out, 16)
                    act_.wait_ge(xnT_ps, r + 1)
                    a.activation(xnT[:, :], ps_small[:, 0:D], ACT.Copy).then_inc(xnT_ok, 1)

            def tile(i, first):
                for jj in range(BPT):
                    j = i * BPT + jj
                    following = block_entry(act_, j + 1)
                    block_out(j, jj, following)
                    if jj > 0:
                        block_T(j - 1, jj - 1, None if first else i - 1)
                    elif not first:
                        block_T(j - 1, BPT - 1, None)
                    if not first:
                        norm_work(jj, i - 1)

            act_.sem_inc(aggT_ok, 2)
            act_.sem_inc(x1_out, 16)
            act_.sem_inc(xn_out, 16)
            tile(0, True)
            with act_.Fori(1, NT) as i:
                tile(i, False)
            block_T(NBLK - 1, BPT - 1, None)
            for jj in range(BPT):
                norm_work(jj, NT - 1)

            act_.wait_ge(acc_zero, NBLK + 2)
            for e in range(NE):
                act_.dma_start(w2_sb[:, e * HC * D:(e + 1) * HC * D].rearrange("p (c n) -> p c n", n=D),
                               W2[e].rearrange("(c p) n -> p c n", p=P)).then_inc(w_in, 16)
            act_.dma_start(b1_bc, b1.rearrange("(o e) n -> o (e n)", o=1).to_broadcast([P, NE * H])
                           ).then_inc(b_in, 16)
            act_.dma_start(b2_bc, b2.rearrange("(o e) n -> o (e n)", o=1).to_broadcast([P, NE * D])
                           ).then_inc(b_in, 16)
            act_.wait_ge(slots_ok, 1)

            def turn_T(k):
                act_.wait_ge(xbT_ps, k + 1)
                if not (isinstance(k, int) and k == 0):
                    act_.wait_ge(hid_ps, k)
                a.activation(xbT, bank[2][:, 0:D], ACT.Copy).then_inc(xbT_ok, 1)

            def turn_of(k, last):
                act_.wait_ge(hid_ok, k + 1)
                if not (isinstance(k, int) and k == 0):
                    act_.wait_ge(actT_ps, k)
                a.activation(act, hid, ACT.Gelu).then_inc(act_ok, 1)
                act_.wait_ge(actT_ps, k + 1)
                if not (isinstance(k, int) and k == 0):
                    act_.wait_ge(y_ps, k)
                a.activation(actT, bank[3][:, 0:H], ACT.Copy).then_inc(actT_ok, 1)
                if last < 2:
                    turn_T(k + 2) if last == 0 else None

            turn_T(0)
            turn_T(1)
            turn_of(0, 0)
            with act_.Fori(1, NFFN - 2) as k:
                turn_of(k, 0)
            turn_of(NFFN - 2, 1)
            turn_of(NFFN - 1, 1)

        @block.vector
        def _(dve):
            v = nc.vector
            own = Tally(dve, dve_own)
            dve.wait_ge(raw_in[0], 48)
            v.tensor_copy(raw_fl[0], raw_i[0]).then_inc(conv, 1)
            dve.wait_ge(raw_in[1], 48)
            v.tensor_copy(raw_fl[1], raw_i[1]).then_inc(conv, 1)

            dve.wait_ge(x_in, 16 * 8)
            dve.wait_ge(pads, 4)

            def statistics(t0):
                for u in range(7):
                    own.mark(v.bn_stats(stats[:, u, :], xin[:, bass.ds(t0 + u, 1), :].rearrange("p a d -> p (a d)")))
                own.settle_apart((pads, 4))
                for u in range(7):
                    own.mark(v.bn_aggr(mv7[:, u, :], stats[:, u, :]))
                own.settle()
                own.mark(v.tensor_copy(mv[:, bass.ds(t0, 7), :], mv7[:, :, :]))
                own.settle()

            assert NT % 7 == 0
            with dve.Fori(0, NT // 7) as i:
                own.enter(i, 15)
                statistics(i * 7)
                own.leave(NT // 7)
            v.tensor_scalar(mv[:, :, 1], mv[:, :, 1], EPS, None, ALU.add).then_inc(var_ok, 1)
            dve.wait_ge(std_ok, 1)
            v.reciprocal(rs[:, :], rs[:, :]).then_inc(rs_ok, 1)
            dve.wait_ge(rs_ok, 1)
            for n in range(NT // 2):
                v.tensor_scalar(xin[:, n, :], xin[:, n, :], mv[:, n, 0:1], rs[:, n:n + 1],
                                ALU.subtract, ALU.mult).then_inc(norm_d, 1)

            dve.wait_ge(conv, 2)
            own.mark(v.tensor_copy(end_i[:, :], raw_fl[1].rearrange("p (c e) -> p c e", e=P)[:, :, P - 1]))
            own.mark(v.tensor_copy(div_f[:, 0, 0:1], part[:, 0:1]))
            own.mark(v.memset(ones16[:, :], 1.0))
            own.settle()
            own.mark(v.tensor_scalar(end_i[:, :], end_i[:, :], 4, None, ALU.arith_shift_right))
            own.mark(v.tensor_scalar(tile_id[:, :], nodes[:, 0:NCOL], float(P), div_f[:, 0, 0:1], ALU.mult, ALU.add))
            own.mark(v.tensor_scalar(block_id[:, :], nodes[:, 0:4], float(JC), div_f[:, 0, 0:1], ALU.mult, ALU.add))
            own.settle()
            v.tensor_copy(end_b[:, :], end_i[:, :]).then_inc(passed_ok, 1)
            dve.wait_ge(passed_ok, 1)
            for c in range(NCOL):
                v.tensor_scalar(passed[:, c, :], nodes[:, 0:NB1], end_b[:, c:c + 1], None, ALU.is_gt
                                ).then_inc(passed_ok, 1)

            def whole_steps(to, x, rows, cols):
                q, over, qi = div_f[0:rows, 1, 0:cols], div_f[0:rows, 2, 0:cols], div_i[0:rows, 0:cols]
                own.mark(v.tensor_scalar(q, x, 0.5, 1.0 / STEP, ALU.add, ALU.mult))
                own.settle()
                own.mark(v.tensor_copy(qi, q))
                own.settle()
                own.mark(v.tensor_copy(q, qi))
                own.settle()
                own.mark(v.scalar_tensor_tensor(over, q, float(STEP), x, ALU.mult, ALU.is_gt))
                own.settle()
                own.mark(v.tensor_tensor(to, q, over, ALU.subtract))
                own.settle()

            dve.wait_ge(first_ok, 1)
            own.mark(v.tensor_copy(ends_of[:, 0, :], bank[5][0:JC, 0:4]))
            own.settle()
            own.mark(v.scalar_tensor_tensor(ends_of[:, 1, :], bank[5][0:JC, 4:8], float(NTILE - 1),
                                            ends_of[:, 0, :], ALU.min, ALU.subtract))
            own.settle()
            whole_steps(steps_of[:, :], ends_of[:, 1, :], JC, 4)
            own.mark(v.tensor_scalar(steps_of[:, :], steps_of[:, :], 1.0, None, ALU.add))
            own.settle()
            for k in range(4):
                v.tensor_scalar(below[:, k, :], nodes[0:JC, 0:NB1], block_id[0:JC, k:k + 1], steps_of[:, k:k + 1],
                                ALU.is_gt, ALU.mult).then_inc(below_ok, 1)
            dve.wait_ge(Q_ok, 1)
            own.mark(v.tensor_copy(first_tile, bank[4][:, 0:NB1]))
            own.settle()
            own.mark(v.tensor_scalar(first_row, first_tile[0:1, :], float(NTILE - 1), None, ALU.min))
            own.mark(v.scalar_tensor_tensor(offset, bank[6][:, 0:NB1], -float(STEP), first_tile, ALU.mult, ALU.add))
            own.settle()
            v.scalar_tensor_tensor(block_tab[0:1, :], bank[6][0:1, 0:NB1], float(CODE), first_row,
                                   ALU.mult, ALU.add).then_inc(tables, 1)
            for c in range(NCOL):
                own.mark(v.scalar_tensor_tensor(pick_scr[:, (3 + c % 2) * NB1:(4 + c % 2) * NB1], nodes[:, 0:NB1],
                                                end_b[:, c:c + 1], offset, ALU.is_equal, ALU.mult,
                                                accum_out=div_f[:, 0, c:c + 1]))
                own.settle()
            own.mark(v.tensor_tensor(div_f[:, 0, :], tile_id[:, :], div_f[:, 0, :], ALU.subtract))
            own.settle()
            whole_steps(last_step[:, :], div_f[:, 0, :], P, NCOL)
            v.tensor_scalar(last_step[:, :], last_step[:, :], 2.0, None, ALU.add).then_inc(last_ok, 1)
            dve.wait_ge(free_ps, 1)
            for n in range(0, NCOL, 4):
                w = min(4, NCOL - n) * P
                of = bank[n // 4][0:1, 0:w].rearrange("p (m u) -> p m u", u=2)[:, :, 1]
                v.tensor_copy(free_at[0:1, n * P // 2:(n * P + w) // 2], of).then_inc(tables, 1)

            own.mark(v.tensor_scalar(part[:, 1:2], part[:, 0:1], R - 1, None, ALU.bitwise_and))
            own.settle()
            own.mark(v.tensor_copy(partf[:, :], part[:, 1:2]))
            own.settle()
            dve.wait_ge(batch_out, len(batches))

            def type_onehot(g, par, turn, quarters, first):
                dve.wait_ge(type_in[par], turn * 64 + 16 * quarters)
                if not first:
                    dve.wait_ge(coef_ps, g)
                v.tensor_scalar(onehot, types[par], partf[:, 0:1], None, ALU.is_equal).then_inc(oh_ok, 1)

            def coefficients(g, par, quarters, ms):
                dve.wait_ge(coef_ps, g + 1)
                to = coef[:, bass.ds(g * (GT * B), quarters * ms * B)].rearrange(
                    "p (q m b) -> p q m b", q=quarters, b=B)
                w = wT[:, bass.ds(g * GT, quarters * ms)].rearrange("p (q m o) -> p q m o", q=quarters, o=1)
                of = bank[par][:, :].rearrange("p (m q b) -> p q m b", q=4, b=B)[:, 0:quarters, 0:ms, :]
                v.tensor_tensor(to, of, w.to_broadcast([P, quarters, ms, B]), ALU.mult).then_inc(coef_ok, 1)

            type_onehot(0, 0, 0, 4, True)
            coefficients(0, 0, 4, GM)
            type_onehot(1, 1, 0, 4, False)
            coefficients(1, 1, 4, GM)
            with dve.Fori(1, NGRP // 2 - 1) as i:
                for par in range(2):
                    type_onehot(i * 2 + par, par, i, 4, False)
                    coefficients(i * 2 + par, par, 4, GM)
            type_onehot(NGRP - 2, 0, NGRP // 2 - 1, 4, False)
            coefficients(NGRP - 2, 0, 4, GM)
            type_onehot(NGRP - 1, 1, NGRP // 2 - 1, 1, False)
            rest = NTILE - (NGRP - 1) * GT
            assert rest <= GM
            coefficients(NGRP - 1, 1, 1, rest)

            own.mark(v.memset(coef[:, NTILE * B:], 0.0))
            own.mark(v.memset(ps_slot[:, :], 0.0))
            own.mark(v.tensor_scalar(count[:, :], nodes[:, 0:NE], float(PER_E * P), None, ALU.mult))
            own.mark(v.tensor_copy(token[:, 0:1], part[:, 0:1]))
            dve.wait_ge(small_in, 96)
            dve.wait_ge(coef_ok, NGRP)
            own.settle()

            def build(j, jj, before, entry, following):
                window = nodes[:, bass.ds(j * WIN, WIN)].rearrange("p (o n) -> p o n", o=1).to_broadcast([P, B, WIN])
                with dve.Fori(entry[0], following[0]) as g:
                    first = tile_of(dve, g, entry)
                    done = dve.snap(((before + (g > entry[0]) * (g - before)) & (CODE - 1)) + 1)
                    for u in range(STEP):
                        if u % 2 == 0:
                            dve.wait_ge(S_used[u // 2], done)
                        c = coef[:, bass.ds((first + u) * B, B)].rearrange("p (b o) -> p b o", o=1)
                        op = v.scalar_tensor_tensor(
                            S[:, jj % 2 * STEP + u, :].rearrange("p (b n) -> p b n", n=WIN), window,
                            dstT[:, bass.ds(first + u, 1)], c.to_broadcast([P, B, WIN]),
                            ALU.is_equal, ALU.mult)
                        if u % 2 == 1:
                            op.then_inc(S_ok[u // 2], 1)

            def norm_work(jj, r):
                if jj == 2:
                    dve.wait_ge(xf_ok, r + 1)
                    dve.wait_ge(xt_in, r * 16 + 16)
                    dve.wait_ge(x1_out, r * 16 + 16)
                    v.scalar_tensor_tensor(x1[:, :], ps_node[:, 0:D], 0.0, xt[:, :], ALU.max, ALU.add
                                           ).then_inc(x1_ok, 1)
                    dve.wait_ge(x1_ok, r + 2)
                    own.mark(v.bn_stats(bst[:, :], x1[:, :]))
                if jj == 3:
                    own.settle_apart((tables, 5))
                    v.bn_aggr(bmv[:, :], bst[:, :]).then_inc(var2_ok, 1)
                if jj == 4:
                    dve.wait_ge(sd_ok, r + 1)
                    own.mark(v.reciprocal(brs[:, 1:2], brs[:, 0:1]))
                    own.settle()
                    dve.wait_ge(xn_out, r * 16 + 16)
                    v.tensor_scalar(xn[:, :], x1[:, :], bmv[:, 0:1], brs[:, 1:2], ALU.subtract, ALU.mult
                                    ).then_inc(xn_ok, 1)
                if jj == 7:
                    dve.wait_ge(gate_ps, r + 1)
                    own.mark(v.tensor_tensor(gate[:, 0, :], ps_small[:, D:D + NE], bg_sb[:, :], ALU.add))
                    own.settle_apart((tables, 5))
                    own.mark(v.max(gate[:, 1, :], gate[:, 0, :]))

            def route_work(jj, r):
                if jj == 0:
                    own.settle_apart((tables, 5))
                    own.mark(v.max_index(top[:, :], gate[:, 1, :], gate[:, 0, :]))
                    own.settle()
                    ids = nodes[:, 0:NE].rearrange("p (o e) -> p o e", o=1).to_broadcast([P, 2, NE])
                    best = top[:, 0:2].rearrange("p (c o) -> p c o", o=1).to_broadcast([P, 2, NE])
                    own.mark(v.tensor_tensor(pick[:, 0:2, :], ids, best, ALU.is_equal))
                if jj == 1:
                    own.settle()
                    v.tensor_tensor(pick[:, 2, :], pick[:, 0, :], pick[:, 1, :], ALU.add).then_inc(pick_ok, 1)
                if jj == 3:
                    dve.wait_ge(rank_ps, r + 1)
                    own.mark(v.tensor_tensor(place[:, :], ps_small[:, 272:272 + NE], count[:, :], ALU.add))
                    own.settle()
                    own.mark(v.tensor_tensor(count[:, :], ps_small[:, 288:288 + NE], count[:, :], ALU.add))
                    to = place[:, :].rearrange("p (o e) -> p o e", o=1).to_broadcast([P, 2, NE])
                    own.mark(v.tensor_tensor(picked[:, :, :], to, pick[:, 0:2, :], ALU.mult))
                if jj == 4:
                    own.settle()
                    own.mark(v.tensor_reduce(slot[:, 0, :], picked[:, :, :], AX.X, ALU.add))
                    own.settle()
                    own.mark(v.tensor_scalar(slot[:, 1, :], slot[:, 0, :], 0.5 - P / 2, 1.0 / P, ALU.add, ALU.mult))
                if jj == 5:
                    own.settle()
                    own.mark(v.tensor_scalar(slot[:, 2, :], slot[:, 1, :], ROUND, None, ALU.add))
                    own.mark(v.tensor_scalar(token[:, 1:2], token[:, 0:1], 1.0, None, ALU.add))
                    own.settle()
                    own.mark(v.tensor_scalar(slot[:, 3, :], slot[:, 2, :], -ROUND, -float(P), ALU.add, ALU.mult))
                    own.mark(v.tensor_scalar(token[:, 0:1], token[:, 0:1], float(P), None, ALU.add))
                    dve.wait_ge(map_ok, r + 1)
                    own.mark(v.tensor_scalar(col_id[:, 0, :], nodes[:, 0:NSLOT], ROUND, slot[:, 2, 0:1],
                                             ALU.add, ALU.is_equal))
                    own.settle()
                    own.mark(v.tensor_tensor(slot[:, 4, :], slot[:, 3, :], slot[:, 0, :], ALU.add))
                if jj == 6:
                    own.settle()
                    own.mark(v.tensor_scalar(col_id[:, 1, :], nodes[:, 0:NSLOT], ROUND, slot[:, 2, 1:2],
                                             ALU.add, ALU.is_equal))
                    for c in range(2):
                        own.mark(v.tensor_scalar(slot_oh[:, c, :], nodes[:, 0:P], slot[:, 4, c:c + 1], token[:, 1:2],
                                                 ALU.is_equal, ALU.mult))
                    own.settle()
                    dve.sem_inc(oh2_ok, 1)

            MARKS = 20

            def tile(i, first):
                before = 0 if first else block_entry(dve, i * BPT - 1)[0]
                entry = block_entry(dve, i * BPT)
                for jj in range(BPT):
                    j = i * BPT + jj
                    following = block_entry(dve, j + 1)
                    build(j, jj, before, entry, following)
                    before, entry = entry[0], following
                    if not first:
                        norm_work(jj, i - 1)
                    if not (isinstance(i, int) and i < 2):
                        route_work(jj, i - 2)

            dve.wait_ge(tables, 5)
            dve.sem_inc(x1_ok, 1)
            tile(0, True)
            tile(1, False)
            with dve.Fori(2, NT) as i:
                own.enter(i - 2, MARKS)
                tile(i, False)
                own.leave(NT - 2)
            for jj in range(BPT):
                norm_work(jj, NT - 1)
                route_work(jj, NT - 2)
            for jj in range(BPT):
                route_work(jj, NT - 1)

            dve.wait_ge(map_ok, NT + 1)
            own.mark(v.memset(slot_f[:, :, :], 0.0))
            own.settle()
            own.mark(v.tensor_scalar(slot_f[:, 0, 0:NSLOT], ps_slot[:, 0:NSLOT], -1.0, 0.0, ALU.add, ALU.max))
            own.mark(v.tensor_scalar(slot_f[:, 1, 0:NSLOT], ps_slot[:, 0:NSLOT], 0.0, None, ALU.is_equal))
            own.mark(v.memset(slot_f[:, 1, NSLOT:], 1.0))
            own.settle()
            own.mark(v.tensor_copy(slot_i[:, :, 0], slot_f[:, 0, :]))
            own.mark(v.scalar_tensor_tensor(slot_i[:, :, 1], slot_f[:, 1, :], float(SKIP), slot_f[:, 0, :],
                                            ALU.mult, ALU.add))
            own.mark(v.scalar_tensor_tensor(nb[:, 1, :], nodes[:, 0:NE], -float(PER_E * P), count[:, :],
                                            ALU.mult, ALU.add))
            own.settle()
            own.mark(v.tensor_scalar(nb[:, 0, :], nb[:, 1, :], float(P - 1), None, ALU.add))
            own.settle()
            own.mark(v.tensor_copy(nb_i[:, :], nb[:, 0, :]))
            own.settle()
            own.mark(v.tensor_scalar(nb_i[:, :], nb_i[:, :], 7, None, ALU.arith_shift_right))
            own.settle()
            own.mark(v.tensor_copy(nb[:, 0, :], nb_i[:, :]))
            own.settle()
            own.mark(v.tensor_scalar(nb[:, 2, :], nb[:, 0, :], -1.0, float(PER_E), ALU.mult, ALU.add))
            own.mark(v.tensor_copy(nb[:, 1, 0:1], nb[:, 0, 0:1]))
            own.settle()
            for e in range(1, NE):
                own.mark(v.tensor_tensor(nb[:, 1, e:e + 1], nb[:, 1, e - 1:e], nb[:, 0, e:e + 1], ALU.add))
                own.settle()
            own.mark(v.memset(blkrow[:, 0, :], 0.0))
            own.mark(v.tensor_copy(blkrow[:, 1, :], nodes[:, 0:NFFN]))
            own.settle()
            for e in range(NE):
                own.mark(v.tensor_scalar(blkrow[:, 2, :], nodes[:, 0:NFFN], nb[:, 1, e:e + 1], None, ALU.is_ge))
                own.settle()
                own.mark(v.tensor_tensor(blkrow[:, 0, :], blkrow[:, 0, :], blkrow[:, 2, :], ALU.add))
                own.mark(v.scalar_tensor_tensor(blkrow[:, 1, :], blkrow[:, 2, :], nb[:, 2, e:e + 1],
                                                blkrow[:, 1, :], ALU.mult, ALU.add))
                own.settle()
            own.mark(v.tensor_scalar(blk_e[0:1, :], blkrow[0:1, 0, :], float(NE - 1), None, ALU.min))
            own.settle()
            v.tensor_copy(blk_c[0:1, :], blkrow[0:1, 1, :]).then_inc(slots_ok, 1)
            dve.wait_ge(slots_ok, 1)
            dve.wait_ge(b_in, 32)

            def add_b1(k, e):
                dve.wait_ge(hid_ps, k + 1)
                if not (isinstance(k, int) and k == 0):
                    dve.wait_ge(act_ok, k)
                v.tensor_tensor(hid, bank[0][:, 0:H], b1_bc[:, bass.ds(e * H, H)], ALU.add).then_inc(hid_ok, 1)

            def add_b2(k, par, e):
                dve.wait_ge(y_ps, k + 1)
                if not (isinstance(k, int) and k < 2):
                    dve.wait_ge(y_out, k * 16 - 16)
                v.tensor_tensor(y_sb[par], bank[1][:, 0:D], b2_bc[:, bass.ds(e * D, D)], ALU.add).then_inc(y_ok, 1)

            def expert(k):
                return dve.value_load(blk_e[0:1, bass.ds(k, 1)], min_val=0, max_val=NE - 1)

            def turn_of(k, par):
                add_b1(k + 1, expert(k + 1))
                add_b2(k, par, expert(k))

            add_b1(0, expert(0))
            turn_of(0, 0)
            turn_of(1, 1)
            with dve.Fori(1, NFFN // 2 - 1) as i:
                for par in range(2):
                    turn_of(i * 2 + par, par)
            turn_of(NFFN - 2, 0)
            add_b2(NFFN - 1, 1, expert(NFFN - 1))


_INS = ['x', 'src', 'dst', 'edge_type_32', 'edge_weight1', 'L0_gnn_bases', 'L0_gnn_w_comp', 'L0_ffn_Wg',
        'L0_ffn_bg', 'L0_ffn_W1', 'L0_ffn_b1', 'L0_ffn_W2', 'L0_ffn_b2']


def kernel(**inputs):
    import numpy as _np
    import concourse.bacc as _bacc
    from concourse.bass_utils import run_bass_kernel_spmd as _run

    nc = _bacc.Bacc("TRN2", target_bir_lowering=False, num_devices=1)
    arrays, args = {}, []
    for name in _INS:
        a = _np.ascontiguousarray(inputs[name])
        arrays[f"in_{name}"] = a
        args.append(nc.dram_tensor(f"in_{name}", a.shape, mybir.dt.from_np(a.dtype), kind="ExternalInput").ap())
    out = nc.dram_tensor("out_rows", inputs["x"].shape, F32, kind="ExternalOutput").ap()
    gnn_moe_layer(nc, *args, out)
    r = _run(nc, [arrays], core_ids=[0])
    return r.results[0]["out_rows"]
```

```python
from contextlib import ExitStack

import concourse.bass as bass
from concourse import mybir

P = 128
ALU = mybir.AluOpType
AX = mybir.AxisListType
ACT = mybir.ActivationFunctionType
F32 = mybir.dt.float32
I32 = mybir.dt.int32
U32 = mybir.dt.uint32
U16 = mybir.dt.uint16
BF16 = mybir.dt.bfloat16

EPS = 1e-5
WIN = 16
RING = 16
STEP = 6
CODE = 2048
ROUND = 1.5 * (1 << 23)
LAG = 4
SKIP = 1 << 24


def wait_apart(eng, sem, value, passed_by):
    value = value if isinstance(value, int) else eng.to_reg(value)
    eng.wait_ge(*passed_by)
    eng.wait_ge(sem, value)


class Tally:

    def __init__(self, eng, sem):
        self.eng, self.sem, self.base, self.n = eng, sem, 0, 0

    def mark(self, ins):
        ins.then_inc(self.sem, 1)
        self.n += 1

    def settle(self):
        self.eng.wait_ge(self.sem, self.base + self.n)

    def settle_apart(self, passed_by):
        wait_apart(self.eng, self.sem, self.base + self.n, passed_by)

    def enter(self, turn, per):
        self.start, self.per = self.base + self.n, per
        self.base, self.n = self.start + turn * per, 0

    def leave(self, turns):
        assert self.n == self.per, (self.n, self.per)
        self.base, self.n = self.start + turns * self.per, 0


def gnn_moe_layer(nc, x, src, dst, etype, eweight, bases, w_comp, Wg, bg, W1, b1, W2, b2, out):
    N, D = x.shape
    E = src.shape[0]
    B = bases.shape[0]
    R = w_comp.shape[0]
    NE, _, H = W1.shape
    NT = -(-N // P)
    LAST = N - (NT - 1) * P
    BPT = P // WIN
    NBLK = NT * BPT
    EPAIR = 2 * P
    NPAIR = -(-E // EPAIR)
    NTILE = 2 * NPAIR
    NB1 = NBLK + 2
    JC = NBLK // 4
    QMAX = NBLK + (NTILE + NBLK) // STEP + 1
    NCOL = -(-NTILE // P)
    DH = D // P
    HC = H // P
    CG = 4
    NCG = NCOL // CG
    MS = P // 4
    REST_MG = -(-(NTILE - NCG * CG * P) // 16)
    COEFS = NCG * MS // 4 + REST_MG
    XC = 7
    HOUT = 16 * (-(-N // (XC * P)) + 1)
    GP = 2 * P
    PER_E = -(-N // GP) * 2
    NSLOT = NE * PER_E
    NGROUP = (2 * N + NE * (GP - 1)) // GP + NE
    assert NCG * CG + 1 == NCOL and NT % XC == 0
    assert D == 256 and B * WIN == P and R * 4 == P and NE == 8 and NSLOT <= 512
    assert NE * PER_E * P < 1 << 23 and E < 1 << 24

    h_dram = nc.dram_tensor("h_scratch", (N, D), F32, kind="Internal").ap()
    xn_dram = nc.dram_tensor("xn_scratch", (N, D), F32, kind="Internal").ap()

    with ExitStack() as ctx:
        def sb(name, shape, dt=F32):
            return ctx.enter_context(nc.sbuf_tensor(name, shape, dt))

        def sem(name):
            return ctx.enter_context(nc.semaphore(name))

        psum = ctx.enter_context(nc.psum_tensor("psum", [P, 8, 512], F32))
        bank = [psum[:, n, :] for n in range(8)]
        acc, tr = bank[0:2], bank[2:4]
        ps_node, ps_small, ps_slot = bank[4], bank[5], bank[6]
        ps_h, ps_xT, ps_y = [bank[0], bank[1], bank[4], bank[5]], bank[2], [bank[3], bank[7]]

        bases_sb = sb("bases_sb", [P, B, DH, D])
        ffn_w = sb("ffn_w", [P, NE * DH * H + NE * HC * D])
        w1_sb = ffn_w[:, 0:NE * DH * H]
        w2_sb = ffn_w[:, NE * DH * H:]
        xin = ffn_w[:, 0:NT * D].rearrange("p (t d) -> p t d", d=D)
        WT0 = NE * DH * H + NE * HC * D - NCOL * P
        wT = ffn_w[:, WT0:]
        types_raw = ffn_w[:, NT * D:NT * D + NCOL * P].bitcast(I32)
        assert NT * D + NCOL * P <= WT0
        RING0 = NE * DH * H
        ring = ffn_w[:, RING0:RING0 + RING * 2 * D]
        EARLY = (WT0 - RING0) // (2 * D)
        assert RING0 + RING * 2 * D <= NE * DH * H + NE * HC * D

        coef = sb("coef", [P, (NTILE + STEP) * B])
        RAW = NCOL * P
        raw_i = [coef[:, k * RAW:(k + 1) * RAW].bitcast(I32) for k in range(2)]
        raw_f = [coef[:, k * RAW:(k + 1) * RAW] for k in range(2, 5)]
        passed = coef[:, 5 * RAW:5 * RAW + NCOL * NB1 // 2].bitcast(BF16).rearrange("p (c j) -> p c j", j=NB1)
        BELOW0 = 5 * RAW + NCOL * NB1 // 2
        below = coef[0:JC, BELOW0:BELOW0 + 4 * NB1].rearrange("p (c j) -> p c j", j=NB1)
        assert BELOW0 + 4 * NB1 <= NTILE * B
        used = [0]

        def late(n):
            used[0] += n
            assert used[0] <= NTILE * B
            return coef[:, used[0] - n:used[0]]

        b2_bc, b1_rows, b1T = late(NE * D), late(P), late(NE * HC)
        xb, xbT, hid, y_sb = late(2 * D), late(DH * GP), late(HC * GP), late(2 * D)
        slot_f = late(2 * NSLOT).rearrange("p (o c) -> p o c", o=2)
        slot_i = late(2 * NSLOT).bitcast(I32).rearrange("p (o c) -> p o c", o=2)
        group_e = late(3 * (NGROUP + 2) * NE).rearrange("p (o g e) -> p o g e", o=3, e=NE)
        cum_e = late(3 * NE * NE).rearrange("p (o f e) -> p o f e", o=3, e=NE)

        dstT = sb("dstT", [P, NCOL * P])
        srcT = sb("srcT", [P, NCOL * P], I32)
        nodes = sb("nodes", [P, NBLK * WIN], U16)
        S = sb("S", [P, 2 * STEP, P])
        blk = sb("blk", [P, 2, D])
        aggT = sb("aggT", [P, DH * B * P])
        pick_scr = aggT[:, 0:5 * NB1]
        bases_flat = bases_sb[:, :, :, :].rearrange("p b h o -> p (b h o)")
        SPREAD = (P + 12) * R
        spread = bases_flat[:, 0:SPREAD // 2].bitcast(BF16)
        types = bases_flat[:, SPREAD // 2:SPREAD // 2 + NCOL * P // 2].bitcast(BF16)
        OH0 = SPREAD // 2 + NCOL * P // 2
        onehot = [bases_flat[:, OH0 + n * CG * P // 2:OH0 + (n + 1) * CG * P // 2].bitcast(BF16) for n in range(4)]
        assert OH0 + 2 * CG * P <= B * DH * D
        spread_sb = [aggT[:, n * CG * P // 2:(n + 1) * CG * P // 2].bitcast(BF16) for n in range(4)]
        sums = aggT[:, 2 * CG * P:3 * CG * P]
        idx = sb("idx", [P, 2, 2 * RING], I32)
        ident = sb("ident", [P, P])
        lower = sb("lower", [P, P])
        ones = sb("ones", [P, P])
        zeros = sb("zeros", [P, D])
        comp4 = sb("comp4", [P, 4 * B])
        comp_rest = sb("comp_rest", [P, 3, 4 * B])
        comp_parts = sb("comp_parts", [P, 3, 4 * B], BF16)
        part = sb("part", [P, 2], I32)
        partf = sb("partf", [P, 2])
        end_i = sb("end_i", [P, NCOL], I32)
        end_b = sb("end_b", [P, NCOL])
        tile_id = sb("tile_id", [P, NCOL])
        block_id = sb("block_id", [P, 4])
        steps_of = sb("steps_of", [JC, 4])
        offset = pick_scr[:, 0:NB1]
        first_tile, first_row = pick_scr[:, NB1:2 * NB1], pick_scr[0:1, 2 * NB1:3 * NB1]
        ends_of = sb("ends_of", [JC, 2, 4])
        div_f = sb("div_f", [P, 3, NCOL])
        div_i = sb("div_i", [P, NCOL], I32)
        last_step = sb("last_step", [P, NCOL])
        steps_tab = sb("steps_tab", [1, NT * 16], U16)
        begin_tab = sb("begin_tab", [1, NT * 16], U16)
        free_at = sb("free_at", [1, NCOL * P // 2], I32)
        ones16 = sb("ones16", [P, P], BF16)
        stats = sb("stats", [P, 2, XC, 6])
        mv = sb("mv", [P, NT, 2])
        rs = sb("rs", [P, NT])
        shift = sb("shift", [P, NT])
        xt = sb("xt", [P, D])
        x1 = sb("x1", [P, D])
        xn = sb("xn", [P, D])
        xnT = sb("xnT", [P, D])
        bst = sb("bst", [P, 6])
        bmv = sb("bmv", [P, 2])
        brs = sb("brs", [P, 2])
        Wg_sb = sb("Wg_sb", [P, DH, NE])
        bg_sb = sb("bg_sb", [P, NE])
        gate = sb("gate", [P, 2, NE])
        top = sb("top", [P, NE], U32)
        pick = sb("pick", [P, 3, NE])
        count = sb("count", [P, NE])
        place = sb("place", [P, NE])
        picked = sb("picked", [P, 2, NE])
        slot = sb("slot", [P, 5, 2])
        eps = sb("eps", [P, 1])
        slot_oh = sb("slot_oh", [P, 2, P])
        col_id = sb("col_id", [P, 2, NSLOT])
        token = sb("token", [P, 2])
        groups = sb("groups", [P, 5, NE])
        groups_i = sb("groups_i", [P, NE], I32)
        group_f = sb("group_f", [1, NGROUP + 2])
        group_col = sb("group_col", [1, NGROUP + 2], I32)
        group_end = sb("group_end", [1, NE], I32)
        gidx = sb("gidx", [P, 2], I32)
        sidx = sb("sidx", [P, 2], I32)

        pads = sem("pads")
        raw_in = [sem(f"raw_in{k}") for k in range(4)]
        x_in = [sem(f"x_in{k}") for k in range(NT // XC)]
        consts = sem("consts")
        small_in = sem("small_in")
        bases_in = sem("bases_in")
        conv = sem("conv")
        batch = sem("batch")
        batch_out = sem("batch_out")
        var_ok, std_ok, rs_ok = sem("var_ok"), sem("std_ok"), sem("rs_ok")
        norm_ok = sem("norm_ok")
        h_out = sem("h_out")
        passed_ok, first_ok = sem("passed_ok"), sem("first_ok")
        below_ok, Q_ok, last_ok, free_ps = sem("below_ok"), sem("Q_ok"), sem("last_ok"), sem("free_ps")
        tables = sem("tables")
        types_ok = sem("types_ok")
        spread_ok = sem("spread_ok")
        bc_ok = sem("bc_ok")
        oh_ok = sem("oh_ok")
        oh_used = sem("oh_used")
        sums_ok = sem("sums_ok")
        coef_ok = sem("coef_ok")
        w_in, b_in = sem("w_in"), sem("b_in")
        idx_ok = sem("idx_ok")
        ring_in = [sem(f"ring_in{k}") for k in range(RING)]
        gathered = sem("gathered")
        released = sem("released")
        S_ok = [sem(f"S_ok{k}") for k in range(STEP // 2)]
        S_used = [sem(f"S_used{k}") for k in range(STEP // 2)]
        blk_ok = sem("blk_ok")
        acc_zero = sem("acc_zero")
        tr_ok, aggT_ok = sem("tr_ok"), sem("aggT_ok")
        xf_ok = sem("xf_ok")
        xt_in, x1_ok, x1_out = sem("xt_in"), sem("x1_ok"), sem("x1_out")
        var2_ok, sd_ok, xn_ok, xn_out = sem("var2_ok"), sem("sd_ok"), sem("xn_ok"), sem("xn_out")
        xnT_ps, xnT_ok, gate_ps = sem("xnT_ps"), sem("xnT_ok"), sem("gate_ps")
        pick_ok, rank_ps, oh2_ok, map_ok = sem("pick_ok"), sem("rank_ps"), sem("oh2_ok"), sem("map_ok")
        dve_own, pool_own = sem("dve_own"), sem("pool_own")
        slots_ok = sem("slots_ok")
        g_idx_ok, s_idx_ok = sem("g_idx_ok"), sem("s_idx_ok")
        xb_in = [sem("xb_in0"), sem("xb_in1")]
        b1_ps, b1_ok = sem("b1_ps"), sem("b1_ok")
        xbT_ps, xbT_ok = sem("xbT_ps"), sem("xbT_ok")
        hid_ps, hid_ok = sem("hid_ps"), sem("hid_ok")
        y_ps, y_ok = sem("y_ps"), sem("y_ok")
        y_out = sem("y_out")

        block = ctx.enter_context(nc.Block())

        e_full = (E // (P * P)) * P * P
        e_rows = (E - e_full) // P
        e_rest = E - e_full - e_rows * P
        lists = [src, dst, eweight.rearrange("e o -> (e o)"), etype]
        raw_to = [raw_i[0], raw_i[1], raw_f[2], types_raw]
        raw_fl = [raw_f[0], raw_f[1], raw_f[2]]
        batches = [(k, c, min(4, NCOL - c)) for k in range(3) for c in range(0, NCOL, 4)]

        def entries(eng, i):
            def load(table, n, high):
                _, values = nc.values_load_multi_w_load_instructions(
                    table[0:1, bass.ds(i * 16, n)], engines=[eng.engine], min_val=0, max_val=high,
                    skip_runtime_bounds_check_because="uint16 that count steps and tiles")
                return values
            done, begin = load(steps_tab, BPT + 2, QMAX), load(begin_tab, BPT, CODE - 1)
            return [(done[jj], done[jj + 1], done[jj + 2], begin[jj]) for jj in range(BPT)]

        def tile_of(eng, step, begin):
            return nc.s_assert_within(eng.snap((step * STEP + begin) % CODE), 0, NTILE - 1,
                                      skip_runtime_bounds_check_because="the last step begins at a tile that exists")

        def last_group(eng, e):
            end = nc.values_load(group_end[0:1, e:e + 1], engines=[eng.engine], min_val=0, max_val=NGROUP,
                                 skip_runtime_bounds_check_because="it counts groups that exist")
            return eng.snap(end & (CODE - 1))

        def steps_of_tile(r):
            return LAST if isinstance(r, int) and r == NT - 1 else P

        @block.sync
        def _(sp):
            sp.wait_ge(pads, 5)
            for k in range(4):
                to = raw_to[k].rearrange("p (c e) -> p c e", e=P)
                c = e_full // (P * P)
                sp.dma_start(to[:, 0:c, :], lists[k][0:e_full].rearrange("(c p e) -> p c e", p=P, e=P)
                             ).then_inc(raw_in[k], 16)
                sp.dma_start(to[0:e_rows, c, :], lists[k][e_full:E - e_rest].rearrange("(p e) -> p e", e=P)
                             ).then_inc(raw_in[k], 16)
                sp.dma_start(to[e_rows:e_rows + 1, c, 0:e_rest],
                             lists[k][E - e_rest:E].rearrange("(o e) -> o e", o=1)).then_inc(raw_in[k], 16)
            for n in range(NT // XC - 1):
                sp.dma_start(xin[:, n * XC:(n + 1) * XC, :],
                             x[n * XC * P:(n + 1) * XC * P, :].rearrange("(t p) d -> p t d", p=P)).then_inc(x_in[n], 16)
            sp.dma_start(xin[:, NT - XC:NT - 1, :],
                         x[(NT - XC) * P:(NT - 1) * P, :].rearrange("(t p) d -> p t d", p=P)).then_inc(x_in[-1], 16)
            sp.dma_start(xin[0:LAST, NT - 1, :], x[(NT - 1) * P:N, :]).then_inc(x_in[-1], 16)
            sp.wait_ge(consts, 7)
            for q in range(4):
                sp.dma_start(comp4[R * q:R * q + R, B * q:B * q + B], w_comp).then_inc(small_in, 16)
            sp.dma_start(Wg_sb[:, :, :], Wg.rearrange("(h p) e -> p h e", p=P)).then_inc(small_in, 16)
            sp.dma_start(bg_sb[:, :], bg.rearrange("(o e) -> o e", o=1).to_broadcast([P, NE])
                         ).then_inc(small_in, 16)
            for n in range(NT // XC):
                sp.wait_ge(norm_ok, (n + 1) * XC)
                full = min((n + 1) * XC, NT - 1)
                sp.dma_start(h_dram[n * XC * P:full * P, :].rearrange("(t p) d -> p t d", p=P),
                             xin[:, n * XC:full, :]).then_inc(h_out, 16)
            sp.dma_start(h_dram[(NT - 1) * P:N, :], xin[0:LAST, NT - 1, :]).then_inc(h_out, 16)
            def relay(slot, turn, m, lagged):
                sp.wait_ge(ring_in[slot], turn * 32 + 32)
                sp.sem_inc(gathered, 2)
                if lagged:
                    at = sp.value_load(free_at[0:1, bass.ds(m - LAG, 1)], min_val=1, max_val=QMAX + 1)
                    sp.wait_ge(S_used[-1], at)
                    sp.sem_inc(released, 1)

            sp.wait_ge(tables, 6)
            for m in range(RING):
                relay(m, 0, m, m >= LAG)
            with sp.Fori(1, NPAIR // RING) as turn:
                for k in range(RING):
                    relay(k, turn, turn * RING + k, True)
            for k in range(NPAIR % RING):
                relay(k, NPAIR // RING, NPAIR // RING * RING + k, True)
            sp.sem_inc(gathered, STEP)

        @block.gpsimd
        def _(pool):
            g = nc.gpsimd
            for k, v in ((0, 0), (1, NBLK * WIN - 1)):
                g.memset(raw_i[k][:, (NCOL - 1) * P:], v).then_inc(pads, 1)
            g.memset(raw_f[2][:, (NCOL - 1) * P:], 0.0).then_inc(pads, 1)
            g.memset(xin[:, NT - 1, :], 0.0).then_inc(pads, 1)
            g.memset(types_raw[:, (NCOL - 1) * P:], 0).then_inc(pads, 1)
            g.memset(ones[:, :], 1.0).then_inc(pool_own, 1)
            g.memset(zeros[:, :], 0.0).then_inc(consts, 1)
            g.memset(comp4[:, :], 0.0).then_inc(consts, 1)
            g.memset(eps[:, :], EPS).then_inc(consts, 1)
            g.iota(nodes[:, :], [[1, NBLK * WIN]], base=0, channel_multiplier=0).then_inc(consts, 1)
            g.iota(part[:, 0:1], [[0, 1]], base=0, channel_multiplier=1).then_inc(consts, 1)
            pool.wait_ge(pool_own, 1)
            g.affine_select(out=ident[:, :], in_=ones[:, :], compare_op=ALU.is_equal, fill=0.0, base=0,
                            pattern=[[-1, P]], channel_multiplier=1).then_inc(consts, 1)
            g.affine_select(out=lower[:, :], in_=ones[:, :], compare_op=ALU.is_gt, fill=0.0, base=0,
                            pattern=[[1, P]], channel_multiplier=-1).then_inc(consts, 1)
            pool.wait_ge(batch_out, len([0 for k, _, _ in batches if k == 0]))
            pool.wait_ge(h_out, HOUT)
            turns = NPAIR // (2 * RING)

            def gathers(half, m0, n, copies, first):
                if not first:
                    pool.wait_ge(released, m0 - RING + 1)
                g.tensor_copy(idx[:, half, 0:2 * n], srcT[:, bass.ds(m0 * 2, 2 * n)]).then_inc(idx_ok, 1)
                wait_apart(pool, idx_ok, copies + 1, (h_out, HOUT))
                for k in range(n):
                    if first and k == EARLY:
                        pool.wait_ge(coef_ok, COEFS)
                    if not first:
                        wait_apart(pool, released, m0 + k - RING + 1, (h_out, HOUT))
                    for t in range(2):
                        at = (k * 2 + t) * D
                        g.indirect_dma_start(
                            out=ring[:, at:at + D], out_offset=None, in_=h_dram,
                            in_offset=bass.IndirectOffsetOnAxis(ap=idx[:, half, 2 * k + t:2 * k + t + 1], axis=0)
                        ).then_inc(ring_in[k], 16)

            gathers(0, 0, RING, 0, True)
            gathers(1, RING, RING, 1, False)
            with pool.Fori(1, turns) as turn:
                gathers(0, turn * 2 * RING, RING, turn * 2, False)
                gathers(1, turn * 2 * RING + RING, RING, turn * 2 + 1, False)
            rest = NPAIR - turns * 2 * RING
            assert 0 < rest <= RING
            gathers(0, turns * 2 * RING, rest, turns * 2, False)

            pool.wait_ge(slots_ok, 1)
            pool.wait_ge(xn_out, 16 * NT + 16)
            pool.wait_ge(x1_out, 16 * NT + 16)

            def add_rows(h, rows):
                g.indirect_dma_start(
                    out=out, out_offset=bass.IndirectOffsetOnAxis(ap=sidx[:, h:h + 1], axis=0), in_=rows,
                    in_offset=None, bounds_check=N - 1, oob_is_err=False, compute_op=ALU.add).then_inc(y_out, 16)

            def slots(to, which, k, done, ready, after=None):
                c = nc.values_load(group_col[0:1, bass.ds(k, 1)], engines=[pool.engine], min_val=0,
                                   max_val=NSLOT - 2,
                                   skip_runtime_bounds_check_because="it is held below the last column")
                if after:
                    pool.wait_ge(*after)
                g.tensor_copy(to[:, :], slot_i[:, which, bass.ds(c, 2)]).then_inc(done, 1)
                wait_apart(pool, done, ready, (slots_ok, 1))

            def fetch(k, after=None):
                slots(gidx, 0, k, g_idx_ok, k + 1, after)
                for h in range(2):
                    g.indirect_dma_start(
                        out=xb[:, h * D:(h + 1) * D], out_offset=None, in_=xn_dram,
                        in_offset=bass.IndirectOffsetOnAxis(ap=gidx[:, h:h + 1], axis=0)).then_inc(xb_in[h], 16)

            fetch(0)
            g.memset(sidx[:, :], SKIP).then_inc(s_idx_ok, 1)
            pool.wait_ge(s_idx_ok, 1)
            for h in range(2):
                add_rows(h, zeros[:, :])
                pool.wait_ge(y_out, 16 * h + 16)
            fetch(1, (xbT_ps, 1))
            with pool.Fori(0, last_group(pool, NE - 1)) as k:
                fetch(k + 2, (xbT_ps, k + 2))
                slots(sidx, 1, k, s_idx_ok, k + 2, (y_out, k * 32 + 32))
                for h in range(2):
                    wait_apart(pool, y_ok, k * 2 + (3 + h), (slots_ok, 1))
                    if h:
                        wait_apart(pool, y_out, k * 32 + 48, (slots_ok, 1))
                    add_rows(h, y_sb[:, h * D:(h + 1) * D])
            end = last_group(pool, NE - 1)
            pool.wait_ge(y_out, end * 32 + 32)
            for h in range(2):
                pool.wait_ge(xb_in[h], end * 16 + 32)

        @block.tensor
        def _(pe):
            t = nc.tensor
            pe.wait_ge(consts, 7)
            for n, (k, c, w) in enumerate(batches):
                if c == 0:
                    if k < 2:
                        pe.wait_ge(conv, k + 1)
                    else:
                        pe.wait_ge(raw_in[2], 48)
                if n >= 8:
                    pe.wait_ge(batch_out, n - 7)
                for u in range(w):
                    mm = t.transpose(bank[n % 8][:, u * P:(u + 1) * P],
                                     raw_fl[k][:, (c + u) * P:(c + u + 1) * P], ident[:, :])
                mm.then_inc(batch, 1)
            pe.wait_ge(passed_ok, NCOL + 1)
            pe.wait_ge(batch_out, len(batches))
            for c in range(NCOL):
                t.matmul(bank[4][:, 0:NB1], ones16[:, :], passed[:, c, :], start=(c == 0), stop=(c == NCOL - 1))
            for n in range(8):
                k, nxt = n % 4, n // 4
                for c in range(NCOL):
                    mm = t.matmul(bank[5][0:JC, n:n + 1], passed[:, c, k * JC + nxt:(k + 1) * JC + nxt],
                                  ones16[:, 0:1], start=(c == 0), stop=(c == NCOL - 1))
            mm.then_inc(first_ok, 1)
            pe.wait_ge(below_ok, 4)
            for k in range(4):
                mm = t.matmul(bank[6][:, 0:NB1], ones[0:JC, :], below[:, k, :], start=(k == 0), stop=(k == 3))
            mm.then_inc(Q_ok, 1)
            pe.wait_ge(last_ok, 1)
            for c in range(NCOL):
                mm = t.matmul(bank[c // 4][0:1, c % 4 * P:(c % 4 + 1) * P], last_step[:, c:c + 1], ident[:, :],
                              start=True, stop=True)
            mm.then_inc(free_ps, 1)
            pe.wait_ge(types_ok, 3)
            pe.sem_inc(oh_used, 4)
            spread_ps = [bank[0], bank[1], bank[2], bank[7]]

            def spread_types(g, m):
                t.matmul(spread_ps[m], spread[:, bass.ds((g // NCG * 4 + m) * P, P)],
                         types[:, bass.ds(g % NCG * (CG * P), CG * P)], start=True, stop=True).then_inc(spread_ok, 1)

            def comps(to, buf, c):
                return t.matmul(to, onehot[buf][:, c * P:(c + 1) * P],
                                comp_parts[:, :, :].rearrange("p k n -> p (k n)"), start=True, stop=True)

            GROUPS = NCG * MS // 4
            for m in range(3):
                spread_types(0, m)
            with pe.Fori(0, GROUPS) as g:
                for m in range(4):
                    pe.wait_ge(bc_ok, g * 4 + (m + 1))
                    if m == 0:
                        spread_types(g, 3)
                    else:
                        spread_types(g + 1, m - 1)
                    pe.wait_ge(oh_ok, g * 4 + (m + 5))
                    if m == 0:
                        pe.wait_ge(sums_ok, g + 1)
                    for c in range(CG):
                        mm = comps(psum[:, 3 + c, m * P:m * P + 12 * B], m, c)
                    mm.then_inc(oh_used, 1)
            pe.wait_ge(oh_ok, GROUPS * 4 + 5)
            def spread_rest(i):
                for m in range(4):
                    mm = t.matmul(bank[7][:, m * P:(m + 1) * P], spread[:, bass.ds((i * 4 + m) * P, P)],
                                  types[:, NCG * CG * P:], start=True, stop=True)
                mm.then_inc(spread_ok, 1)

            spread_rest(0)
            with pe.Fori(0, REST_MG) as i:
                pe.wait_ge(bc_ok, i + (GROUPS * 4 + 3))
                spread_rest(i + 1)
                pe.wait_ge(oh_ok, i + (GROUPS * 4 + 6))
                pe.wait_ge(sums_ok, i + (GROUPS + 1))
                for m in range(4):
                    mm = comps(bank[3][:, m * P:m * P + 12 * B], 1, m)
                mm.then_inc(oh_used, 1)

            pe.wait_ge(coef_ok, COEFS)
            for used in S_used:
                t.matmul(ps_small[:, 0:NE], ones[:, :], ones[:, 0:NE], start=True, stop=True).then_inc(used, 1)
            pe.wait_ge(tables, 6)

            def steps(j, jj, start, end, begin):
                wait_apart(pe, acc_zero, j + 1, (tables, 6))
                with pe.Fori(start, end) as g:
                    first = tile_of(pe, g, begin)
                    pe.wait_ge(gathered, first + STEP)
                    for u in range(STEP):
                        if u % 2 == 0:
                            pe.wait_ge(S_ok[u // 2], g + 1)
                        mm = t.matmul(acc[jj % 2][:, 0:D], S[:, jj % 2 * STEP + u, :],
                                      ring[:, bass.ds((first + u) % (2 * RING) * D, D)],
                                      start=False, stop=False, skip_group_check=True)
                        if u % 2 == 1:
                            mm.then_inc(S_used[u // 2], 1)

            def turn_block(j, par):
                pe.wait_ge(blk_ok, j + 1)
                pe.wait_ge(aggT_ok, j + 1)
                for h in range(DH):
                    mm = t.transpose(tr[par][:, h * P:(h + 1) * P], blk[:, par, h * P:(h + 1) * P], ident[:, :])
                mm.then_inc(tr_ok, 1)

            def transform(r):
                pe.wait_ge(aggT_ok, r * BPT + BPT + 2)
                pe.wait_ge(x1_ok, r + 1)
                for n in range(B * DH):
                    b, h = n // DH, n % DH
                    mm = t.matmul(ps_node[:, 0:D], aggT[:, (h * B + b) * P:(h * B + b + 1) * P],
                                  bases_sb[:, b, h, :], start=(n == 0), stop=(n == B * DH - 1))
                mm.then_inc(xf_ok, 1)

            def norm_work(jj, r):
                if jj == 5:
                    pe.wait_ge(xn_ok, r + 1)
                    for h in range(DH):
                        mm = t.transpose(ps_small[:, h * P:(h + 1) * P], xn[:, h * P:(h + 1) * P], ident[:, :])
                    mm.then_inc(xnT_ps, 1)
                if jj == 6:
                    pe.wait_ge(xnT_ok, r + 1)
                    for h in range(DH):
                        mm = t.matmul(ps_small[:, D:D + NE], xnT[:, h * P:(h + 1) * P], Wg_sb[:, h, :],
                                      start=(h == 0), stop=(h == DH - 1))
                    mm.then_inc(gate_ps, 1)

            def route_work(jj, r):
                if jj == 2:
                    k = steps_of_tile(r)
                    pe.wait_ge(pick_ok, r + 1)
                    t.matmul(ps_small[:, 272:272 + NE], lower[0:k, :], pick[0:k, 2, :], start=True, stop=True)
                    t.matmul(ps_small[:, 288:288 + NE], ones[0:k, :], pick[0:k, 2, :], start=True, stop=True
                             ).then_inc(rank_ps, 1)
                if jj == 7:
                    k = steps_of_tile(r)
                    pe.wait_ge(oh2_ok, r + 1)
                    for c in range(2):
                        mm = t.matmul(ps_slot[:, 0:NSLOT], slot_oh[0:k, c, :], col_id[0:k, c, :],
                                      start=False, stop=False, skip_group_check=True)
                    mm.then_inc(map_ok, 1)

            def tile(i, first):
                blocks = entries(pe, i)
                for jj in range(BPT):
                    j = i * BPT + jj
                    steps(j, jj, *blocks[jj][1:])
                    if jj == 1 and not first:
                        transform(i - 1)
                    if not (first and jj == 0):
                        turn_block(j - 1, (jj - 1) % 2)
                    if not first:
                        norm_work(jj, i - 1)
                    if not (isinstance(i, int) and i < 2):
                        route_work(jj, i - 2)

            pe.sem_inc(map_ok, 1)
            tile(0, True)
            pe.wait_ge(bases_in, 16)
            tile(1, False)
            with pe.Fori(2, NT) as i:
                tile(i, False)
            turn_block(NBLK - 1, 1)
            route_work(2, NT - 2)
            transform(NT - 1)
            route_work(7, NT - 2)
            for jj in range(BPT):
                norm_work(jj, NT - 1)
            for jj in range(BPT):
                route_work(jj, NT - 1)

            pe.wait_ge(acc_zero, NBLK + 2)
            pe.sem_inc(y_ps, 2)
            pe.wait_ge(b_in, 32)
            t.transpose(ps_y[1][:, 0:NE * HC], b1_rows[0:NE * HC, :], ident[0:NE * HC, 0:NE * HC]).then_inc(b1_ps, 1)
            pe.wait_ge(slots_ok, 1)
            pe.wait_ge(w_in, 32)

            def rows_T(k):
                for h in range(2):
                    pe.wait_ge(xb_in[h], k * 16 + 16)
                for n in range(2 * DH):
                    h, half = n // 2, n % 2
                    mm = t.transpose(ps_xT[:, n * P:(n + 1) * P], xb[:, half * D + h * P:half * D + (h + 1) * P],
                                     ident[:, :])
                mm.then_inc(xbT_ps, 1)

            def up(k, e):
                pe.wait_ge(xbT_ok, k + 1)
                for c in range(HC):
                    for h in range(DH):
                        at = e * DH * H + h * H + c * P
                        mm = t.matmul(ps_h[c][:, 0:GP], w1_sb[:, at:at + P],
                                      xbT[:, h * GP:(h + 1) * GP], start=(h == 0), stop=(h == DH - 1))
                    mm.then_inc(hid_ps, 1)

            def down(k, e):
                for half in range(2):
                    pe.wait_ge(y_ok, k * 2 + (1 + half))
                    for c in range(HC):
                        if half == 0:
                            pe.wait_ge(hid_ok, k * HC + (c + 1))
                        mm = t.matmul(ps_y[half][:, 0:D],
                                      hid[:, c * GP + half * P:c * GP + (half + 1) * P],
                                      w2_sb[:, (e * HC + c) * D:(e * HC + c + 1) * D],
                                      start=(c == 0), stop=(c == HC - 1))
                    mm.then_inc(y_ps, 1)

            rows_T(0)
            start = 0
            for e in range(NE):
                end = last_group(pe, e)
                with pe.Fori(start, end) as k:
                    up(k, e)
                    rows_T(k + 1)
                    down(k, e)
                start = end

        @block.scalar
        def _(act_):
            a = nc.scalar
            act_.wait_ge(consts, 7)
            for n, (k, c, w) in enumerate(batches):
                act_.wait_ge(batch, n + 1)
                to = (srcT, dstT, wT)[k][:, c * P:(c + w) * P]
                a.activation(to, bank[n % 8][:, 0:w * P], ACT.Copy).then_inc(batch_out, 1)
            for n in range(NT // XC):
                part_of = slice(n * XC, (n + 1) * XC)
                act_.wait_ge(var_ok, n + 1)
                a.activation(rs[:, part_of], mv[:, part_of, 1], ACT.Sqrt, bias=eps[:, 0:1]).then_inc(std_ok, 1)
                act_.wait_ge(rs_ok, n + 1)
                for u in range(n * XC, (n + 1) * XC):
                    a.activation(xin[:, u, :], xin[:, u, :], ACT.Identity, bias=shift[:, u:u + 1],
                                 scale=rs[:, u:u + 1]).then_inc(norm_ok, 1)
            act_.wait_ge(types_ok, 3)
            act_.sem_inc(bc_ok, 1)
            GROUPS = NCG * MS // 4

            def copy_types(s, m, extra=0):
                act_.wait_ge(spread_ok, s + (1 + extra))
                act_.wait_ge(oh_ok, s + 1)
                a.activation(spread_sb[m], [bank[0], bank[1], bank[2], bank[7]][m], ACT.Copy).then_inc(bc_ok, 1)

            copy_types(0, 0)
            with act_.Fori(0, GROUPS) as g:
                for m in range(4):
                    copy_types(g * 4 + (m + 1), (m + 1) % 4)
            with act_.Fori(0, REST_MG) as i:
                act_.wait_ge(spread_ok, i + (GROUPS * 4 + 4))
                act_.wait_ge(oh_ok, i + (GROUPS * 4 + 5))
                a.activation(spread_sb[1], bank[7], ACT.Copy).then_inc(bc_ok, 1)
            act_.wait_ge(h_out, HOUT)
            act_.wait_ge(coef_ok, COEFS)
            for n in range(2):
                a.activation(acc[n][:, 0:D], zeros[:, :], ACT.Copy).then_inc(acc_zero, 1)
            act_.dma_start(bases_sb[:, :, :, :].rearrange("p b h o -> p (b h) o"),
                           bases.rearrange("b (h p) o -> p (b h) o", p=P)).then_inc(bases_in, 16)
            act_.dma_start(w1_sb.rearrange("p (k n) -> p k n", n=H),
                           W1.rearrange("e (h p) n -> p (e h) n", p=P)).then_inc(w_in, 16)
            act_.wait_ge(tables, 6)

            def block_out(j, jj, end):
                act_.wait_ge(S_used[-1], end + 1)
                if not (isinstance(j, int) and j < 2):
                    act_.wait_ge(tr_ok, j - 1)
                a.activation(blk[:, jj % 2, :], acc[jj % 2][:, 0:D], ACT.Copy).then_inc(blk_ok, 1)
                act_.wait_ge(blk_ok, j + 1)
                a.activation(acc[jj % 2][:, 0:D], zeros[:, :], ACT.Copy).then_inc(acc_zero, 1)

            def block_T(j, jj, prev):
                act_.wait_ge(tr_ok, j + 1)
                if jj == 0 and prev is not None:
                    act_.wait_ge(xf_ok, prev + 1)
                to = aggT[:, :].rearrange("p (g n) -> p g n", n=P)[:, :, jj * WIN:(jj + 1) * WIN]
                a.activation(to, tr[jj % 2][:, 0:D].rearrange("p (g n) -> p g n", n=WIN), ACT.Copy
                             ).then_inc(aggT_ok, 1)

            def norm_work(jj, r):
                k = steps_of_tile(r)
                rows = bass.ds(r * P, k)
                if jj == 0:
                    act_.wait_ge(x1_ok, r + 1)
                    act_.dma_start(xt[0:k, :], x[rows, :]).then_inc(xt_in, 16)
                if jj == 2:
                    act_.wait_ge(x1_ok, r + 2)
                    act_.dma_start(out[rows, :], x1[0:k, :]).then_inc(x1_out, 16)
                if jj == 3:
                    act_.wait_ge(var2_ok, r + 1)
                    a.activation(brs[:, 0:1], bmv[:, 1:2], ACT.Sqrt, bias=eps[:, 0:1]).then_inc(sd_ok, 1)
                if jj == 5:
                    act_.wait_ge(xn_ok, r + 1)
                    act_.dma_start(xn_dram[rows, :], xn[0:k, :]).then_inc(xn_out, 16)
                    act_.wait_ge(xnT_ps, r + 1)
                    a.activation(xnT[:, :], ps_small[:, 0:D], ACT.Copy).then_inc(xnT_ok, 1)

            def tile(i, first):
                blocks = entries(act_, i)
                for jj in range(BPT):
                    j = i * BPT + jj
                    block_out(j, jj, blocks[jj][2])
                    if jj > 0:
                        block_T(j - 1, jj - 1, None if first else i - 1)
                    elif not first:
                        block_T(j - 1, BPT - 1, None)
                    if not first:
                        norm_work(jj, i - 1)

            act_.sem_inc(aggT_ok, 2)
            act_.sem_inc(x1_out, 16)
            act_.sem_inc(xn_out, 16)
            tile(0, True)
            with act_.Fori(1, NT) as i:
                tile(i, False)
            block_T(NBLK - 1, BPT - 1, None)
            for jj in range(BPT):
                norm_work(jj, NT - 1)

            act_.wait_ge(acc_zero, NBLK + 2)
            act_.dma_start(w2_sb.rearrange("p (k n) -> p k n", n=D),
                           W2.rearrange("e (c p) n -> p (e c) n", p=P)).then_inc(w_in, 16)
            act_.dma_start(b1_rows[0:NE * HC, :], b1.rearrange("e (c n) -> (e c) n", n=P)).then_inc(b_in, 16)
            act_.dma_start(b2_bc, b2.rearrange("(o e) n -> o (e n)", o=1).to_broadcast([P, NE * D])
                           ).then_inc(b_in, 16)
            act_.wait_ge(b1_ps, 1)
            a.activation(b1T, ps_y[1][:, 0:NE * HC], ACT.Copy).then_inc(b1_ok, 1)
            act_.wait_ge(b1_ok, 1)
            act_.wait_ge(slots_ok, 1)

            def rows_out(k):
                act_.wait_ge(xbT_ps, k + 1)
                a.activation(xbT, ps_xT[:, 0:DH * GP], ACT.Copy).then_inc(xbT_ok, 1)

            rows_out(0)
            start = 0
            for e in range(NE):
                end = last_group(act_, e)
                with act_.Fori(start, end) as k:
                    act_.wait_ge(y_ps, k * 2 + 2)
                    for c in range(HC):
                        wait_apart(act_, hid_ps, k * HC + (c + 1), (slots_ok, 1))
                        a.activation(hid[:, c * GP:(c + 1) * GP], ps_h[c][:, 0:GP],
                                     ACT.Gelu, bias=b1T[:, e * HC + c:e * HC + c + 1]).then_inc(hid_ok, 1)
                    rows_out(k + 1)
                start = end

        @block.vector
        def _(dve):
            v = nc.vector
            own = Tally(dve, dve_own)
            dve.wait_ge(raw_in[0], 48)
            v.tensor_copy(raw_fl[0], raw_i[0]).then_inc(conv, 1)
            dve.wait_ge(raw_in[1], 48)
            v.tensor_copy(raw_fl[1], raw_i[1]).then_inc(conv, 1)

            def statistics(n):
                dve.wait_ge(x_in[n], 32 if n == NT // XC - 1 else 16)
                if n > 1:
                    dve.wait_ge(var_ok, n - 1)
                for u in range(XC):
                    own.mark(v.bn_stats(stats[:, n % 2, u, :], xin[:, n * XC + u, :]))
                own.settle()
                for u in range(XC):
                    op = v.bn_aggr(mv[:, n * XC + u, :], stats[:, n % 2, u, :])
                op.then_inc(var_ok, 1)

            def scales(n):
                part_of = slice(n * XC, (n + 1) * XC)
                dve.wait_ge(std_ok, n + 1)
                own.mark(v.reciprocal(rs[:, part_of], rs[:, part_of]))
                own.settle()
                v.scalar_tensor_tensor(shift[:, part_of], mv[:, part_of, 0], -1.0, rs[:, part_of],
                                       ALU.mult, ALU.mult).then_inc(rs_ok, 1)

            dve.wait_ge(consts, 7)
            own.mark(v.tensor_scalar(part[:, 1:2], part[:, 0:1], R - 1, None, ALU.bitwise_and))
            own.mark(v.tensor_copy(partf[:, 1:2], part[:, 0:1]))
            own.settle()
            own.mark(v.tensor_copy(partf[:, 0:1], part[:, 1:2]))
            of = nodes[:, 0:P + 12].rearrange("p (i o) -> p i o", o=1).to_broadcast([P, P + 12, R])
            v.tensor_scalar(spread.rearrange("p (i r) -> p i r", r=R), of, partf[:, 1:2], None, ALU.is_equal
                            ).then_inc(types_ok, 1)
            dve.wait_ge(raw_in[3], 48)
            v.tensor_copy(types, types_raw).then_inc(types_ok, 1)
            dve.wait_ge(conv, 2)
            dve.wait_ge(consts, 7)
            own.mark(v.tensor_copy(end_i[:, :], raw_fl[1].rearrange("p (c e) -> p c e", e=P)[:, :, P - 1]))
            own.mark(v.tensor_copy(div_f[:, 0, 0:1], part[:, 0:1]))
            own.mark(v.memset(ones16[:, :], 1.0))
            own.settle()
            own.mark(v.tensor_scalar(end_i[:, :], end_i[:, :], 4, None, ALU.arith_shift_right))
            own.mark(v.tensor_scalar(tile_id[:, :], nodes[:, 0:NCOL], float(P), div_f[:, 0, 0:1], ALU.mult, ALU.add))
            own.mark(v.tensor_scalar(block_id[:, :], nodes[:, 0:4], float(JC), div_f[:, 0, 0:1], ALU.mult, ALU.add))
            own.settle()
            v.tensor_copy(end_b[:, :], end_i[:, :]).then_inc(passed_ok, 1)
            dve.wait_ge(passed_ok, 1)
            for c in range(NCOL):
                v.tensor_scalar(passed[:, c, :], nodes[:, 0:NB1], end_b[:, c:c + 1], None, ALU.is_gt
                                ).then_inc(passed_ok, 1)

            def whole_steps(to, x, rows, cols):
                q, over, qi = div_f[0:rows, 1, 0:cols], div_f[0:rows, 2, 0:cols], div_i[0:rows, 0:cols]
                own.mark(v.tensor_scalar(q, x, 0.5, 1.0 / STEP, ALU.add, ALU.mult))
                own.settle()
                own.mark(v.tensor_copy(qi, q))
                own.settle()
                own.mark(v.tensor_copy(q, qi))
                own.settle()
                own.mark(v.scalar_tensor_tensor(over, q, float(STEP), x, ALU.mult, ALU.is_gt))
                own.settle()
                own.mark(v.tensor_tensor(to, q, over, ALU.subtract))
                own.settle()

            statistics(0)
            statistics(1)
            scales(0)
            dve.wait_ge(first_ok, 1)
            own.mark(v.tensor_copy(ends_of[:, 0, :], bank[5][0:JC, 0:4]))
            own.settle()
            own.mark(v.scalar_tensor_tensor(ends_of[:, 1, :], bank[5][0:JC, 4:8], float(NTILE - 1),
                                            ends_of[:, 0, :], ALU.min, ALU.subtract))
            own.settle()
            whole_steps(steps_of[:, :], ends_of[:, 1, :], JC, 4)
            own.mark(v.tensor_scalar(steps_of[:, :], steps_of[:, :], 1.0, None, ALU.add))
            own.settle()
            for k in range(4):
                v.tensor_scalar(below[:, k, :], nodes[0:JC, 0:NB1], block_id[0:JC, k:k + 1], steps_of[:, k:k + 1],
                                ALU.is_gt, ALU.mult).then_inc(below_ok, 1)
            statistics(2)
            scales(1)
            statistics(3)
            scales(2)
            dve.wait_ge(Q_ok, 1)
            own.mark(v.tensor_copy(first_tile, bank[4][:, 0:NB1]))
            own.settle()
            own.mark(v.scalar_tensor_tensor(offset, bank[6][:, 0:NB1], -float(STEP), first_tile, ALU.mult, ALU.add))
            own.settle()
            own.mark(v.tensor_scalar(first_row.bitcast(I32), offset[0:1, :], float(STEP * CODE), None, ALU.add))
            own.settle()
            own.mark(v.tensor_scalar(first_row.bitcast(I32), first_row.bitcast(I32), CODE - 1, None, ALU.bitwise_and))
            own.settle()
            by_tile = lambda row, at: row[0:1, at:at + NT * BPT].rearrange("p (i k) -> p i k", k=BPT)
            to_steps = steps_tab[:, :].rearrange("p (i k) -> p i k", k=16)
            v.tensor_copy(begin_tab[:, :].rearrange("p (i k) -> p i k", k=16)[:, :, 0:BPT],
                          by_tile(first_row.bitcast(I32), 0)).then_inc(tables, 1)
            own.mark(v.memset(steps_tab[:, :], 0))
            own.settle()
            own.mark(v.tensor_copy(to_steps[:, :, 1:BPT + 1], by_tile(bank[6], 0)))
            own.mark(v.tensor_copy(to_steps[:, 1:, 0], by_tile(bank[6], BPT - 1)[:, 0:NT - 1, 0]))
            v.tensor_copy(to_steps[:, :, BPT + 1], by_tile(bank[6], BPT - 8 + 1)[:, :, BPT - 1]).then_inc(tables, 1)
            own.settle()
            for c in range(NCOL):
                own.mark(v.scalar_tensor_tensor(pick_scr[:, (3 + c % 2) * NB1:(4 + c % 2) * NB1], nodes[:, 0:NB1],
                                                end_b[:, c:c + 1], offset, ALU.is_equal, ALU.mult,
                                                accum_out=div_f[:, 0, c:c + 1]))
                own.settle()
            own.mark(v.tensor_tensor(div_f[:, 0, :], tile_id[:, :], div_f[:, 0, :], ALU.subtract))
            own.settle()
            whole_steps(last_step[:, :], div_f[:, 0, :], P, NCOL)
            v.tensor_scalar(last_step[:, :], last_step[:, :], 2.0, None, ALU.add).then_inc(last_ok, 1)
            for n in range(4, NT // XC):
                statistics(n)
                scales(n - 1)
            scales(NT // XC - 1)
            dve.wait_ge(free_ps, 1)
            for n in range(0, NCOL, 4):
                w = min(4, NCOL - n) * P
                of = bank[n // 4][0:1, 0:w].rearrange("p (m u) -> p m u", u=2)[:, :, 1]
                v.tensor_copy(free_at[0:1, n * P // 2:(n * P + w) // 2], of).then_inc(tables, 1)

            dve.wait_ge(small_in, 96)
            own.mark(v.tensor_copy(comp_parts[:, 0, :], comp4[:, :]))
            own.settle()
            for k in range(2):
                own.mark(v.tensor_copy(comp_rest[:, 2, :], comp_parts[:, k, :]))
                own.settle()
                own.mark(v.tensor_tensor(comp_rest[:, k, :], comp_rest[:, k - 1, :] if k else comp4[:, :],
                                         comp_rest[:, 2, :], ALU.subtract))
                own.settle()
                op = v.tensor_copy(comp_parts[:, k + 1, :], comp_rest[:, k, :])
                if k == 0:
                    own.mark(op)
                    own.settle()
            op.then_inc(types_ok, 1)
            dve.wait_ge(batch_out, len(batches))
            dve.sem_inc(oh_ok, 4)
            dve.sem_inc(sums_ok, 1)

            def type_onehot(s, m, used):
                dve.wait_ge(bc_ok, s + 2)
                dve.wait_ge(oh_used, used + 1)
                v.tensor_scalar(onehot[m], spread_sb[m], partf[:, 0:1], None, ALU.is_equal).then_inc(oh_ok, 1)

            def sum_parts(done, g, products, n):
                dve.wait_ge(oh_used, done)
                if not (isinstance(g, int) and g == 0):
                    dve.wait_ge(coef_ok, g)
                v.tensor_reduce(sums[:, 0:n].rearrange("p (m n) -> p m n", n=4 * B), products, AX.X, ALU.add
                                ).then_inc(sums_ok, 1)

            def coefficients(g, coefs, weights, shape, n):
                dve.wait_ge(sums_ok, g + 2)
                v.tensor_tensor(coefs, sums[:, 0:n].rearrange("p (c t b) -> p c t b", t=16, b=B),
                                weights.to_broadcast(shape), ALU.mult).then_inc(coef_ok, 1)

            GROUPS = NCG * MS // 4
            wT_by = wT[:, 0:NCG * CG * P].rearrange("p (c t) -> p c t", t=P)
            coef_by = coef[:, 0:NCG * CG * P * B].rearrange("p (c t) -> p c t", t=P * B)
            products = psum[:, 3:3 + CG, :].rearrange("p c (m k n) -> p (c m) n k", k=4, n=4 * B)[:, :, :, 0:3]

            def coefficients_of(g):
                mg, cg = g // NCG, g % NCG
                coefficients(g, coef_by[:, bass.ds(cg * CG, CG), bass.ds(mg * (16 * B), 16 * B)].rearrange(
                                 "p c (t b) -> p c t b", b=B),
                             wT_by[:, bass.ds(cg * CG, CG), bass.ds(mg * 16, 16)].rearrange(
                                 "p c (t o) -> p c t o", o=1), [P, CG, 16, B], CG * P)

            def group(g, first):
                for m in range(1, 4):
                    type_onehot(g * 4 + m, m, g * 4 + m)
                if not first:
                    coefficients_of(g - 1)
                type_onehot(g * 4 + 4, 0, g * 4 + 4)
                sum_parts(g * 4 + 8, g, products, CG * P)

            type_onehot(0, 0, 0)
            group(0, True)
            with dve.Fori(1, GROUPS) as g:
                group(g, False)
            coefficients_of(GROUPS - 1)
            with dve.Fori(0, REST_MG) as i:
                dve.wait_ge(bc_ok, i + (GROUPS * 4 + 3))
                dve.wait_ge(oh_used, i + (GROUPS * 4 + 4))
                v.tensor_scalar(onehot[1], spread_sb[1], partf[:, 0:1], None, ALU.is_equal).then_inc(oh_ok, 1)
                at = NCG * CG * P
                sum_parts(i + (GROUPS * 4 + 5), i + GROUPS, products[:, 0:4, :, :], P)
                coefficients(i + GROUPS,
                             coef[:, bass.ds(i * (16 * B) + at * B, 16 * B)].rearrange(
                                 "p (c t b) -> p c t b", c=1, b=B),
                             wT[:, bass.ds(i * 16 + at, 16)].rearrange("p (c t o) -> p c t o", c=1, o=1),
                             [P, 1, 16, B], P)
            dve.wait_ge(coef_ok, COEFS)

            own.mark(v.memset(coef[:, NTILE * B:], 0.0))
            own.mark(v.memset(ps_slot[:, :], 0.0))
            own.mark(v.tensor_scalar(count[:, :], nodes[:, 0:NE], float(PER_E * P), None, ALU.mult))
            own.mark(v.tensor_copy(token[:, 0:1], part[:, 0:1]))
            dve.wait_ge(small_in, 96)
            dve.wait_ge(coef_ok, COEFS)
            own.settle()

            def build(j, jj, before, start, end, begin):
                window = nodes[:, bass.ds(j * WIN, WIN)].rearrange("p (o n) -> p o n", o=1).to_broadcast([P, B, WIN])
                with dve.Fori(start, end) as g:
                    first = tile_of(dve, g, begin)
                    done = dve.snap((g > start) * g + (g <= start) * before + 1)
                    for u in range(STEP):
                        if u % 2 == 0:
                            dve.wait_ge(S_used[u // 2], done)
                        c = coef[:, bass.ds((first + u) * B, B)].rearrange("p (b o) -> p b o", o=1)
                        op = v.scalar_tensor_tensor(
                            S[:, jj % 2 * STEP + u, :].rearrange("p (b n) -> p b n", n=WIN), window,
                            dstT[:, bass.ds(first + u, 1)], c.to_broadcast([P, B, WIN]),
                            ALU.is_equal, ALU.mult)
                        if u % 2 == 1:
                            op.then_inc(S_ok[u // 2], 1)

            def norm_work(jj, r):
                if jj == 2:
                    dve.wait_ge(xf_ok, r + 1)
                    dve.wait_ge(xt_in, r * 16 + 16)
                    dve.wait_ge(x1_out, r * 16 + 16)
                    v.scalar_tensor_tensor(x1[:, :], ps_node[:, 0:D], 0.0, xt[:, :], ALU.max, ALU.add
                                           ).then_inc(x1_ok, 1)
                    dve.wait_ge(x1_ok, r + 2)
                    own.mark(v.bn_stats(bst[:, :], x1[:, :]))
                if jj == 3:
                    own.settle_apart((tables, 6))
                    v.bn_aggr(bmv[:, :], bst[:, :]).then_inc(var2_ok, 1)
                if jj == 4:
                    dve.wait_ge(sd_ok, r + 1)
                    own.mark(v.reciprocal(brs[:, 1:2], brs[:, 0:1]))
                    own.settle()
                    dve.wait_ge(xn_out, r * 16 + 16)
                    v.tensor_scalar(xn[:, :], x1[:, :], bmv[:, 0:1], brs[:, 1:2], ALU.subtract, ALU.mult
                                    ).then_inc(xn_ok, 1)
                if jj == 7:
                    dve.wait_ge(gate_ps, r + 1)
                    own.mark(v.tensor_tensor(gate[:, 0, :], ps_small[:, D:D + NE], bg_sb[:, :], ALU.add))
                    own.settle_apart((tables, 6))
                    own.mark(v.max(gate[:, 1, :], gate[:, 0, :]))

            def route_work(jj, r):
                if jj == 0:
                    own.settle_apart((tables, 6))
                    own.mark(v.max_index(top[:, :], gate[:, 1, :], gate[:, 0, :]))
                    own.settle()
                    ids = nodes[:, 0:NE].rearrange("p (o e) -> p o e", o=1).to_broadcast([P, 2, NE])
                    best = top[:, 0:2].rearrange("p (c o) -> p c o", o=1).to_broadcast([P, 2, NE])
                    own.mark(v.tensor_tensor(pick[:, 0:2, :], ids, best, ALU.is_equal))
                if jj == 1:
                    own.settle()
                    v.tensor_tensor(pick[:, 2, :], pick[:, 0, :], pick[:, 1, :], ALU.add).then_inc(pick_ok, 1)
                if jj == 3:
                    dve.wait_ge(rank_ps, r + 1)
                    own.mark(v.tensor_tensor(place[:, :], ps_small[:, 272:272 + NE], count[:, :], ALU.add))
                    own.settle()
                    own.mark(v.tensor_tensor(count[:, :], ps_small[:, 288:288 + NE], count[:, :], ALU.add))
                    to = place[:, :].rearrange("p (o e) -> p o e", o=1).to_broadcast([P, 2, NE])
                    own.mark(v.tensor_tensor(picked[:, :, :], to, pick[:, 0:2, :], ALU.mult))
                if jj == 4:
                    own.settle()
                    own.mark(v.tensor_reduce(slot[:, 0, :], picked[:, :, :], AX.X, ALU.add))
                    own.settle()
                    own.mark(v.tensor_scalar(slot[:, 1, :], slot[:, 0, :], 0.5 - P / 2, 1.0 / P, ALU.add, ALU.mult))
                if jj == 5:
                    own.settle()
                    own.mark(v.tensor_scalar(slot[:, 2, :], slot[:, 1, :], ROUND, None, ALU.add))
                    own.mark(v.tensor_scalar(token[:, 1:2], token[:, 0:1], 1.0, None, ALU.add))
                    own.settle()
                    own.mark(v.tensor_scalar(slot[:, 3, :], slot[:, 2, :], -ROUND, -float(P), ALU.add, ALU.mult))
                    own.mark(v.tensor_scalar(token[:, 0:1], token[:, 0:1], float(P), None, ALU.add))
                    dve.wait_ge(map_ok, r + 1)
                    own.mark(v.tensor_scalar(col_id[:, 0, :], nodes[:, 0:NSLOT], ROUND, slot[:, 2, 0:1],
                                             ALU.add, ALU.is_equal))
                    own.settle()
                    own.mark(v.tensor_tensor(slot[:, 4, :], slot[:, 3, :], slot[:, 0, :], ALU.add))
                if jj == 6:
                    own.settle()
                    own.mark(v.tensor_scalar(col_id[:, 1, :], nodes[:, 0:NSLOT], ROUND, slot[:, 2, 1:2],
                                             ALU.add, ALU.is_equal))
                    for c in range(2):
                        own.mark(v.tensor_scalar(slot_oh[:, c, :], nodes[:, 0:P], slot[:, 4, c:c + 1], token[:, 1:2],
                                                 ALU.is_equal, ALU.mult))
                    own.settle()
                    dve.sem_inc(oh2_ok, 1)

            MARKS = 20

            def tile(i, first):
                blocks = entries(dve, i)
                for jj in range(BPT):
                    j = i * BPT + jj
                    build(j, jj, *blocks[jj])
                    if not first:
                        norm_work(jj, i - 1)
                    if not (isinstance(i, int) and i < 2):
                        route_work(jj, i - 2)

            dve.wait_ge(tables, 6)
            dve.sem_inc(x1_ok, 1)
            tile(0, True)
            tile(1, False)
            with dve.Fori(2, NT) as i:
                own.enter(i - 2, MARKS)
                tile(i, False)
                own.leave(NT - 2)
            for jj in range(BPT):
                route_work(jj, NT - 2)
            for jj in range(BPT):
                norm_work(jj, NT - 1)
            for jj in range(BPT):
                route_work(jj, NT - 1)

            dve.wait_ge(map_ok, NT + 1)
            own.mark(v.tensor_scalar(slot_f[:, 0, :], ps_slot[:, 0:NSLOT], -1.0, 0.0, ALU.add, ALU.max))
            own.mark(v.tensor_scalar(slot_f[:, 1, :], ps_slot[:, 0:NSLOT], 0.0, float(SKIP), ALU.is_equal, ALU.mult))
            own.mark(v.scalar_tensor_tensor(groups[:, 0, :], nodes[:, 0:NE], -float(PER_E * P), count[:, :],
                                            ALU.mult, ALU.add))
            ids = nodes[:, 0:NE]
            by_row = ids.rearrange("p (f o) -> p f o", o=1).to_broadcast([P, NE, NE])
            by_col = ids.rearrange("p (o e) -> p o e", o=1).to_broadcast([P, NE, NE])
            own.mark(v.tensor_tensor(cum_e[:, 0, :, :], by_row, by_col, ALU.is_ge))
            own.settle()
            own.mark(v.tensor_copy(slot_i[:, 0, :], slot_f[:, 0, :]))
            own.mark(v.tensor_tensor(slot_i[:, 1, :], slot_f[:, 0, :], slot_f[:, 1, :], ALU.add))
            own.mark(v.tensor_scalar(groups[:, 1, :], groups[:, 0, :], float(GP - 1), None, ALU.add))
            own.settle()
            own.mark(v.tensor_copy(groups_i[:, :], groups[:, 1, :]))
            own.settle()
            own.mark(v.tensor_scalar(groups_i[:, :], groups_i[:, :], 8, None, ALU.arith_shift_right))
            own.settle()
            own.mark(v.tensor_scalar(groups[:, 2, :], groups_i[:, :], 1.0, None, ALU.max))
            own.settle()
            n_of = groups[:, 2, :].rearrange("p (o e) -> p o e", o=1).to_broadcast([P, NE, NE])
            own.mark(v.tensor_tensor(cum_e[:, 1, :, :], cum_e[:, 0, :, :], n_of, ALU.mult))
            own.mark(v.tensor_scalar(groups[:, 4, :], groups[:, 2, :], -2.0, float(PER_E), ALU.mult, ALU.add))
            own.settle()
            own.mark(v.tensor_reduce(groups[:, 3, :], cum_e[:, 1, :, :], AX.X, ALU.add))
            own.settle()
            own.mark(v.tensor_copy(group_end[:, :], groups[0:1, 3, :]))
            G = NGROUP + 2
            number = nodes[0:1, 0:G].rearrange("p (g o) -> p g o", o=1).to_broadcast([1, G, NE])
            ends = groups[0:1, 3, :].rearrange("p (o e) -> p o e", o=1).to_broadcast([1, G, NE])
            rests = groups[0:1, 4, :].rearrange("p (o e) -> p o e", o=1).to_broadcast([1, G, NE])
            own.mark(v.tensor_tensor(group_e[0:1, 0, :, :], number, ends, ALU.is_ge))
            own.settle()
            own.mark(v.tensor_tensor(group_e[0:1, 1, :, :], group_e[0:1, 0, :, :], rests, ALU.mult))
            own.settle()
            own.mark(v.tensor_reduce(group_f[:, :], group_e[0:1, 1, :, :], AX.X, ALU.add))
            own.settle()
            own.mark(v.scalar_tensor_tensor(group_f[:, :], nodes[0:1, 0:G], 2.0, group_f[:, :], ALU.mult, ALU.add))
            own.settle()
            v.tensor_scalar(group_col[:, :], group_f[:, :], float(NSLOT - 2), None, ALU.min).then_inc(slots_ok, 1)
            dve.wait_ge(slots_ok, 1)
            dve.wait_ge(b_in, 32)

            start = 0
            dve.sem_inc(y_ok, 2)
            for e in range(NE):
                end = last_group(dve, e)
                with dve.Fori(start, end) as k:
                    for h in range(2):
                        wait_apart(dve, y_ps, k * 2 + (3 + h), (slots_ok, 1))
                        wait_apart(dve, y_out, k * 32 + (16 + 16 * h), (slots_ok, 1))
                        v.tensor_tensor(y_sb[:, h * D:(h + 1) * D], ps_y[h][:, 0:D],
                                        b2_bc[:, e * D:(e + 1) * D], ALU.add).then_inc(y_ok, 1)
                start = end


_INS = ['x', 'src', 'dst', 'edge_type_32', 'edge_weight1', 'L0_gnn_bases', 'L0_gnn_w_comp', 'L0_ffn_Wg',
        'L0_ffn_bg', 'L0_ffn_W1', 'L0_ffn_b1', 'L0_ffn_W2', 'L0_ffn_b2']


def kernel(**inputs):
    import numpy as _np
    import concourse.bacc as _bacc
    from concourse.bass_utils import run_bass_kernel_spmd as _run

    nc = _bacc.Bacc("TRN2", target_bir_lowering=False, num_devices=1)
    arrays, args = {}, []
    for name in _INS:
        a = _np.ascontiguousarray(inputs[name])
        arrays[f"in_{name}"] = a
        args.append(nc.dram_tensor(f"in_{name}", a.shape, mybir.dt.from_np(a.dtype), kind="ExternalInput").ap())
    out = nc.dram_tensor("out_rows", inputs["x"].shape, F32, kind="ExternalOutput").ap()
    gnn_moe_layer(nc, *args, out)
    r = _run(nc, [arrays], core_ids=[0])
    return r.results[0]["out_rows"]
```
